# Optimizing a Trainium2 kernel written in Bass

```python
import numpy as np
import jax
import jax.numpy as jnp

def _softmax(x, axis=-1):
    return jax.nn.softmax(x, axis=axis)

def _gelu(x):
    return jax.nn.gelu(x, approximate=True)

def _silu(x):
    return jax.nn.silu(x)

def _sigmoid(x):
    return jax.nn.sigmoid(x)

def _layernorm(x, axis=-1, eps=1e-05):
    m = jnp.mean(x, axis=axis, keepdims=True)
    v = jnp.var(x, axis=axis, keepdims=True)
    return (x - m) / jnp.sqrt(v + eps)

def _scatter_add(tgt, idx, src, axis=0):
    return tgt.at[idx].add(src)

def _segment_sum(src, seg, n):
    return jax.ops.segment_sum(src, seg, n)
kernel_name = 'mk_gnn_preln_d2_gnn_r32_e38fb3'

def setup_inputs(seed: int=0):
    np.random.seed(seed)
    _w = jnp.asarray

    def _rec_inputs():
        import jax
        import jax.numpy as jnp
        _gk = jax.random.key(seed)
        x = -0.0003713 + 1 * jax.random.normal(jax.random.fold_in(_gk, 1), (3125, 128), jnp.float32)
        _s = jax.random.randint(jax.random.fold_in(_gk, 2), (50000,), 0, 3125, jnp.int32)
        _d = jax.random.randint(jax.random.fold_in(_gk, 3), (50000,), 0, 3125, jnp.int32)
        _loop = jnp.arange(3125, dtype=jnp.int32)
        src = jnp.concatenate([_s, _d, _loop])
        dst = jnp.concatenate([_d, _s, _loop])
        _o = jnp.argsort(dst, stable=True)
        src = src[_o]
        dst = dst[_o]
        edge_type_8 = jax.random.randint(jax.random.fold_in(_gk, 12), (103125,), 0, 8, jnp.int32)
        return (x, src, dst, edge_type_8)
    x, src, dst, edge_type_8 = _rec_inputs()

    def _L0_gnn_setup():
        import jax, jax.numpy as jnp
        import numpy as np
        N_NODES = 3125
        N_EDGES = 50000
        D_IN = 128
        D_H = 128
        EPS = 1e-12

        def _sage_conv_max(x, src, dst, W_l, W_r, b, num_nodes):
            msgs = x[src]
            aggr = jax.ops.segment_max(msgs, dst, num_segments=num_nodes)
            aggr = jnp.where(jnp.isfinite(aggr), aggr, 0.0)
            out = aggr @ W_l + b + x @ W_r
            norm = jnp.linalg.norm(out, axis=-1, keepdims=True)
            return out / jnp.maximum(norm, EPS)
        key = jax.random.key(seed)
        ks = jax.random.split(key, 8)
        s = 1.0 / np.sqrt(D_IN)
        x = jax.random.normal(ks[0], (N_NODES, D_IN), dtype=jnp.float32)
        edge_index = jax.random.randint(ks[1], (2, N_EDGES), 0, N_NODES, dtype=jnp.int64)
        W_l1 = jax.random.uniform(ks[2], (D_IN, D_H), jnp.float32, -s, s)
        W_r1 = jax.random.uniform(ks[3], (D_IN, D_H), jnp.float32, -s, s)
        b1 = jnp.zeros((D_H,), jnp.float32)
        W_l2 = jax.random.uniform(ks[4], (D_H, D_H), jnp.float32, -s, s)
        W_r2 = jax.random.uniform(ks[5], (D_H, D_H), jnp.float32, -s, s)
        b2 = jnp.zeros((D_H,), jnp.float32)
        return {'x': x, 'edge_index': edge_index, 'W_l1': W_l1, 'W_r1': W_r1, 'b1': b1, 'W_l2': W_l2, 'W_r2': W_r2, 'b2': b2}
    _L0_gnn_all = _L0_gnn_setup()
    _L0_gnn_in = {k: v for k, v in _L0_gnn_all.items() if k in ('W_l1', 'W_r1', 'b1', 'W_l2', 'W_r2', 'b2')}
    del _L0_gnn_all

    def _L1_gnn_setup():
        import jax, jax.numpy as jnp
        import numpy as np
        N_ENT = 3125

        def _rgcn_layer(x, W, SW, b, src, dst, rel):
            xt = jnp.einsum('nd,rde->rne', x, W)
            msg = xt[rel, src]
            agg = jax.ops.segment_sum(msg, dst, num_segments=x.shape[0])
            return jax.nn.relu(agg + x @ SW + b)
        key = jax.random.key(seed)
        ks = jax.random.split(key, 8)
        d, R, E = (128, 8, 18750)
        scale = 1.0 / np.sqrt(d)
        return {'entity_emb': jax.random.normal(ks[0], (N_ENT, d), dtype=jnp.float32), 'w1': jax.random.normal(ks[1], (R, d, d), dtype=jnp.float32) * scale, 'sl1': jax.random.normal(ks[2], (d, d), dtype=jnp.float32) * scale, 'b1': jnp.zeros((d,), dtype=jnp.float32), 'w2': jax.random.normal(ks[3], (R, d, d), dtype=jnp.float32) * scale, 'sl2': jax.random.normal(ks[4], (d, d), dtype=jnp.float32) * scale, 'b2': jnp.zeros((d,), dtype=jnp.float32), 'edge_index': jax.random.randint(ks[5], (2, E), 0, N_ENT, dtype=jnp.int64), 'edge_type': jax.random.randint(ks[6], (E,), 0, R, dtype=jnp.int64)}
    _L1_gnn_all = _L1_gnn_setup()
    _L1_gnn_in = {k: v for k, v in _L1_gnn_all.items() if k in ('w1', 'sl1', 'b1', 'w2', 'sl2', 'b2')}
    del _L1_gnn_all
    return {'x': x, 'src': src, 'dst': dst, 'edge_type_8': edge_type_8, 'L0_gnn_W_l1': _L0_gnn_in['W_l1'], 'L0_gnn_W_r1': _L0_gnn_in['W_r1'], 'L0_gnn_b1': _L0_gnn_in['b1'], 'L0_gnn_W_l2': _L0_gnn_in['W_l2'], 'L0_gnn_W_r2': _L0_gnn_in['W_r2'], 'L0_gnn_b2': _L0_gnn_in['b2'], 'L1_gnn_w1': _L1_gnn_in['w1'], 'L1_gnn_sl1': _L1_gnn_in['sl1'], 'L1_gnn_b1': _L1_gnn_in['b1'], 'L1_gnn_w2': _L1_gnn_in['w2'], 'L1_gnn_sl2': _L1_gnn_in['sl2'], 'L1_gnn_b2': _L1_gnn_in['b2']}

def reference(x, src, dst, edge_type_8, L0_gnn_W_l1, L0_gnn_W_r1, L0_gnn_b1, L0_gnn_W_l2, L0_gnn_W_r2, L0_gnn_b2, L1_gnn_w1, L1_gnn_sl1, L1_gnn_b1, L1_gnn_w2, L1_gnn_sl2, L1_gnn_b2):
    import jax
    import jax.numpy as jnp

    def _L0_gnn_ref(x, edge_index, W_l1, W_r1, b1, W_l2, W_r2, b2):
        import jax, jax.numpy as jnp
        import numpy as np
        N_NODES = 3125
        N_EDGES = 50000
        D_IN = 128
        D_H = 128
        EPS = 1e-12

        def _sage_conv_max(x, src, dst, W_l, W_r, b, num_nodes):
            msgs = x[src]
            aggr = jax.ops.segment_max(msgs, dst, num_segments=num_nodes)
            aggr = jnp.where(jnp.isfinite(aggr), aggr, 0.0)
            out = aggr @ W_l + b + x @ W_r
            norm = jnp.linalg.norm(out, axis=-1, keepdims=True)
            return out / jnp.maximum(norm, EPS)
        src, dst = (edge_index[0], edge_index[1])
        h = jax.nn.relu(_sage_conv_max(x, src, dst, W_l1, W_r1, b1, N_NODES))
        h = jax.nn.relu(_sage_conv_max(h, src, dst, W_l2, W_r2, b2, N_NODES))
        return h

    def _L1_gnn_ref(entity_emb, w1, sl1, b1, w2, sl2, b2, edge_index, edge_type):
        import jax, jax.numpy as jnp
        import numpy as np
        N_ENT = 3125

        def _rgcn_layer(x, W, SW, b, src, dst, rel):
            xt = jnp.einsum('nd,rde->rne', x, W)
            msg = xt[rel, src]
            agg = jax.ops.segment_sum(msg, dst, num_segments=x.shape[0])
            return jax.nn.relu(agg + x @ SW + b)
        src, dst = (edge_index[0], edge_index[1])
        x = _rgcn_layer(entity_emb, w1, sl1, b1, src, dst, edge_type)
        x = _rgcn_layer(x, w2, sl2, b2, src, dst, edge_type)
        return x
    edge_index = jnp.stack([src, dst])
    h = jnp.maximum(_layernorm(x, axis=-1), 0.0)
    x = x + _L0_gnn_ref(h, edge_index, L0_gnn_W_l1, L0_gnn_W_r1, L0_gnn_b1, L0_gnn_W_l2, L0_gnn_W_r2, L0_gnn_b2)
    h = jnp.maximum(_layernorm(x, axis=-1), 0.0)
    x = x + _L1_gnn_ref(h, L1_gnn_w1, L1_gnn_sl1, L1_gnn_b1, L1_gnn_w2, L1_gnn_sl2, L1_gnn_b2, edge_index, edge_type_8)
    return x

_drawn_inputs = setup_inputs


def setup_inputs(seed=0):
    import zlib

    import numpy as np

    out = dict(_drawn_inputs(seed))
    spreads = {'L0_gnn_b1': (0.0, 2.0),
     'L0_gnn_b2': (0.0, 0.1),
     'L1_gnn_b1': (0.0, 0.518),
     'L1_gnn_b2': (0.0, 2.0)}
    factors = {'L0_gnn_W_r1': 21.167, 'L0_gnn_W_l1': 5.537, 'L0_gnn_W_r2': 3.08}
    for name, (base, spread) in spreads.items():
        noise = np.random.default_rng([zlib.crc32(name.encode()), seed]).standard_normal(out[name].shape)
        drawn = base * np.exp(spread * noise) if base else spread * noise
        out[name] = jnp.asarray(drawn.astype(out[name].dtype))
    for name, factor in factors.items():
        out[name] = (out[name] * factor).astype(out[name].dtype)
    return out
```

```python
from contextlib import ExitStack

import concourse.bass as bass
from concourse import mybir

F32 = mybir.dt.float32
BF16 = mybir.dt.bfloat16
I32 = mybir.dt.int32
ALU = mybir.AluOpType
ACT = mybir.ActivationFunctionType
AX = mybir.AxisListType

P = 128
D = 128
NODES = 3125
NA, NB = 125, 25
EDGES = 103125
K = -(-EDGES // P)
TAIL = EDGES - (P - 1) * K
RELS = 8
GROUP = 31
SLOTS = 2
TURNS = K // (GROUP * SLOTS)
SUBS = [(0, 8), (8, 8), (16, 8), (24, 7)]
BLK = 5
BLKS = NB // BLK
HI, LO = 49, 64
CLASSES = NODES + 1
REC = 4
EMPTY_ROW = P * K
LN_EPS = 1e-5
NORM_EPS = 1e-12
CREDIT = SLOTS * GROUP
EDGE_CONSTS, CONSTS = 5, 14
N_WEIGHTS = 4 * 2 + 2 + 2
assert K == GROUP * SLOTS * TURNS and NA * NB == NODES and SUBS[-1][0] + SUBS[-1][1] == GROUP


class Steps:

    def __init__(self):
        self.base, self.here, self.i, self.per = 0, 0, None, 0

    def loop(self, i, per):
        self.base, self.here, self.i, self.per = self.base + self.here, 0, i, per

    def end_loop(self, turns):
        assert self.here == self.per, (self.here, self.per)
        self.base, self.here, self.i = self.base + turns * self.per, 0, None

    def next(self):
        self.here += 1
        return self.base + self.here if self.i is None else self.i * self.per + (self.base + self.here)


def build(nc, x, src, dst, edge_type_8, W_l1, W_r1, sb1, W_l2, W_r2, sb2, w1, sl1, rb1, w2, sl2, rb2, out):
    with ExitStack() as ctx:
        def sb(name, shape, dt=F32):
            return ctx.enter_context(nc.sbuf_tensor(name, shape, dt))

        def sem(name):
            return ctx.enter_context(nc.semaphore(name))

        def scratch(name, shape, dt=F32):
            return nc.dram_tensor(name, shape, dt).ap()

        table = [scratch("table0", (NODES, D)), scratch("table1", (NODES, D)),
                 scratch("table2", (NODES * RELS, D)), scratch("table3", (NODES * RELS, D))]
        sorted_d = scratch("sorted_d", (P * K, REC), I32)
        run_rows = [scratch(f"run_rows{l}", (P * K + 1, D)) for l in range(4)]
        end_d, start_d, end_idx_d = scratch("end_d", (HI * LO,)), scratch("start_d", (HI * LO,)), \
            scratch("end_idx_d", (HI * LO,), I32)

        src_t = sb("src_t", [P, K], I32)
        dst_t = sb("dst_t", [P, K], I32)
        typ_t = sb("typ_t", [P, K], I32)
        prev_last = sb("prev_last", [P, 1], I32)
        dst_hi = sb("dst_hi", [P, K], I32)
        dst_lo = sb("dst_lo", [P, K], I32)
        rel_idx = sb("rel_idx", [P, K], I32)
        same = sb("same", [P, K])
        idx_ring = sb("idx_ring", [P, SLOTS, GROUP], I32)
        ring = sb("ring", [P, SLOTS, GROUP, D])
        spare = ring[:, 0, :, :].rearrange("p k d -> p (k d)")
        dst_f = spare[:, 0:K]
        rank = spare[:, K:2 * K]
        hot = spare[:, 2 * K:2 * K + CLASSES // 2].bitcast(BF16)
        x_all = sb("x_all", [NA, NB, D])
        self_all = sb("self_all", [NA, NB, D])
        ends = sb("ends", [NA, NB, D])
        end_idx = sb("end_idx", [NA, NB], I32)
        span = sb("span", [P, NB, NA], BF16)
        end_w = sb("end_w", [P, CLASSES])
        start_w = sb("start_w", [P, CLASSES])
        hit_w = sb("hit_w", [P, K * REC])
        end_b, start_b, hit = end_w[:, 0:NODES], start_w[:, 0:NODES], hit_w[:, 0:NODES]
        before_w = sb("before_w", [P, P], BF16)
        after_w = sb("after_w", [P, P], BF16)
        col = sb("col", [P, 1])
        pos = sb("pos", [P, 1], I32)
        record = sb("record", [P, REC], I32)
        hot_hi = sb("hot_hi", [P, GROUP, HI], BF16)
        hot_lo = sb("hot_lo", [P, GROUP, LO], BF16)
        iota_f = sb("iota_f", [P, LO])
        lo_edge = sb("lo_edge", [P, 1])
        hi_edge = sb("hi_edge", [P, 1])
        ident = sb("ident", [P, P])
        ones = sb("ones", [P, P])
        upper = sb("upper", [HI, HI])
        hist = sb("hist", [HI, LO])
        cum = sb("cum", [HI, LO])
        hist_tmp = sb("hist_tmp", [HI, LO])
        hist_new = sb("hist_new", [HI, LO])
        hist_idx = sb("hist_idx", [HI, LO], I32)
        hist_base = sb("hist_base", [HI, 1])
        zero_row = sb("zero_row", [1, D])
        passes = sb("passes", [P, 1])
        passes_last = sb("passes_last", [P, 1])
        passes_w = sb("passes_w", [P, P])
        passes_b = sb("passes_b", [P, P])
        scr1 = sb("scr1", [P, K])
        unsorted_p = sb("unsorted_p", [P, 2])
        unsorted_i = sb("unsorted_i", [1, 1], I32)
        carry_t = sb("carry_t", [P, P])
        carry = sb("carry", [P, D])
        carry_r = sb("carry_r", [P, D])
        carry_parts = sb("carry_parts", [P, 3, D], BF16)
        last_rows = sb("last_rows", [P, D])
        agg = sb("agg", [NA, BLK, D])
        agg_t = sb("agg_t", [P, BLK, P])
        o_t = sb("o_t", [NA, BLK, D])
        sq_t = sb("sq_t", [NA, BLK, D])
        cen = sb("cen", [NA, BLK, D])
        h_t = sb("h_t", [NA, BLK, D])
        h_tr = sb("h_tr", [P, BLK, P])
        res = sb("res", [NA, BLK, D])
        st = sb("st", [NA, 4, BLK])
        eps_c = sb("eps_c", [NA, 1])
        xt_out = sb("xt_out", [NA, BLK, RELS * D])
        w_l = [None, sb("w_l1", [D, D]), sb("w_l2", [D, D])]
        w_self = [sb(f"w_self{t}", [D, D]) for t in range(4)]
        b_self = [sb(f"b_self{t}", [NA, D]) for t in range(4)]
        w_rel = [None, None, sb("w_rel2", [D, RELS, D]), sb("w_rel3", [D, RELS, D])]

        ps = ctx.enter_context(nc.psum_tensor("ps", [P, 8, 512], F32))
        flat = ps[:, :, :].rearrange("p b n -> p (b n)")
        ps_c = flat[:, 0:BLK * P].rearrange("p (j n) -> p j n", n=P)
        ps_t = flat[:, 1024:1024 + BLK * P].rearrange("p (j n) -> p j n", n=P)
        ps_o = flat[:, 2048:2048 + BLK * P].rearrange("p (j n) -> p j n", n=P)
        ps_xa, ps_xb = ps[:, 6, :], ps[:, 7, :]
        ps_hist = ps[0:HI, 6, 0:LO]
        ps_seen = flat[:, 0:CLASSES]
        ps_small = ps[:, 7, 0:8]

        edges_in = sem("edges_in")
        x_first_in = sem("x_first_in")
        x_in = sem("x_in")
        weights_in = sem("weights_in")
        consts_ready = sem("consts_ready")
        vec = sem("vec")
        unsorted_ready = sem("unsorted_ready")
        check_sum = sem("check_sum")
        check_int = sem("check_int")
        sort_vec = sem("sort_vec")
        sort_begun = sem("sort_begun")
        classes_ready = sem("classes_ready")
        seen_cleared = sem("seen_cleared")
        hot_made = sem("hot_made")
        ranked = sem("ranked")
        rank_read = sem("rank_read")
        counted = sem("counted")
        record_ready = sem("record_ready")
        record_out = sem("record_out")
        record_free = sem("record_free")
        records_in = sem("records_in")
        edges_sorted = sem("edges_sorted")
        idx_ready = sem("idx_ready")
        idx_staged = sem("idx_staged")
        group_begun = sem("group_begun")
        landed = [[sem(f"landed{s}{q}") for q in range(len(SUBS))] for s in range(SLOTS)]
        scan_done = sem("scan_done")
        stored = [sem(f"stored{s}") for s in range(SLOTS)]
        hot_ready = sem("hot_ready")
        hist_part = sem("hist_part")
        hist_added = sem("hist_added")
        base_ready = sem("base_ready")
        tot_ready = sem("tot_ready")
        bounds_ready = sem("bounds_ready")
        bounds_out = sem("bounds_out")
        bounds_in = sem("bounds_in")
        idx_in = sem("idx_in")
        span_ready = sem("span_ready")
        passes_ready = sem("passes_ready")
        passes_bc = sem("passes_bc")
        last_copied = sem("last_copied")
        last_t = sem("last_t")
        carry_scanned = sem("carry_scanned")
        carry_back = sem("carry_back")
        carry_split = sem("carry_split")
        end_row = [sem(f"end_row{j}") for j in range(BLK)]
        zero_out = sem("zero_out")
        c_full = sem("c_full")
        agg_ready = sem("agg_ready")
        agg_t_full = sem("agg_t_full")
        agg_t_sb = sem("agg_t_sb")
        prod_full = sem("prod_full")
        sq_ready = sem("sq_ready")
        root_ready = sem("root_ready")
        h_ready = sem("h_ready")
        h_t_full = sem("h_t_full")
        h_t_sb = sem("h_t_sb")
        self_full = sem("self_full")
        self_sb = sem("self_sb")
        xta_full, xta_sb = sem("xta_full"), sem("xta_sb")
        xtb_full, xtb_sb = sem("xtb_full"), sem("xtb_sb")
        xt_stored = [sem(f"xt_stored{j}") for j in range(BLK)]
        table_out = [sem(f"table_out{t}") for t in range(2)]
        res_ready = sem("res_ready")
        res_out = sem("res_out")

        def run_idx(l):
            return src_t if l < 2 else rel_idx

        def pipeline(eng, turn, steps=None, per=0):
            turn(0, None)
            with eng.Fori(0, BLKS - 1) as u:
                if steps:
                    steps.loop(u, per)
                turn(u + 1, u)
                if steps:
                    steps.end_loop(BLKS - 1)
            turn(None, BLKS - 1)

        def unsorted(eng):
            eng.wait_ge(check_int, 1)
            return eng.value_load(unsorted_i[:, :], min_val=0, max_val=P * K)

        block = ctx.enter_context(nc.Block())

        @block.sync
        def _(sp):
            x_tiles = x.rearrange("(a b) d -> a b d", b=NB)
            sp.dma_start(x_all[:, 0:BLK, :], x_tiles[:, 0:BLK, :]).then_inc(x_first_in, 16)
            sp.dma_start(x_all[:, BLK:NB, :], x_tiles[:, BLK:NB, :]).then_inc(x_in, 16)
            sp.wait_ge(consts_ready, EDGE_CONSTS)
            for tile, d in ((dst_t, dst), (src_t, src), (typ_t, edge_type_8)):
                sp.dma_start(tile[0:P - 1, :], d[0:(P - 1) * K].rearrange("(p k) -> p k", k=K)).then_inc(edges_in, 16)
                sp.dma_start(tile[P - 1:P, 0:TAIL], d[(P - 1) * K:EDGES].rearrange("(p k) -> p k", p=1)).then_inc(edges_in, 16)
            sp.dma_start(prev_last[1:P, :], dst[0:(P - 1) * K].rearrange("(p k) -> p k", k=K)[:, K - 1:K],
                         allow_slow_non_contiguous=True).then_inc(edges_in, 16)
            for t, (w, b) in enumerate(((W_r1, sb1), (W_r2, sb2), (sl1, rb1), (sl2, rb2))):
                sp.dma_start(w_self[t][:, :], w).then_inc(weights_in, 16)
                sp.dma_start(b_self[t][:, :], b.rearrange("(o d) -> o d", o=1).broadcast_to([NA, D])).then_inc(weights_in, 16)
            for t, w in ((1, W_l1), (2, W_l2)):
                sp.dma_start(w_l[t][:, :], w).then_inc(weights_in, 16)
            for t, w in ((2, w1), (3, w2)):
                sp.dma_start(w_rel[t][:, :, :], w.rearrange("r d e -> d r e")).then_inc(weights_in, 16)
            for l in range(4):
                sp.dma_start(run_rows[l][EMPTY_ROW:EMPTY_ROW + 1, :], zero_row[:, :]).then_inc(zero_out, 16)

            def store_h(t):
                tab = table[t].rearrange("(a b) d -> a b d", b=NB)
                with sp.Fori(0, BLKS) as i:
                    sp.wait_ge(h_ready, i + (BLKS * t + 1))
                    sp.dma_start(tab[:, bass.ds(i * BLK, BLK), :], h_t[:, :, :]).then_inc(table_out[t], 16)

            def store_runs(l, first=0, last=TURNS):
                rows = run_rows[l][0:P * K, :].rearrange("(p k) d -> p k d", k=K)
                with sp.Fori(first, last) as i:
                    for s in range(SLOTS):
                        for k0, kn in SUBS:
                            at = s * GROUP + k0
                            sp.wait_ge(scan_done, i * (SLOTS * GROUP) + (CREDIT + K * l + at + kn))
                            sp.dma_start(rows[:, bass.ds(i * (SLOTS * GROUP) + at, kn), :],
                                         ring[:, s, k0:k0 + kn, :]).then_inc(stored[s], 16)

            def store_xt(t):
                tab = table[t].rearrange("(a b r) d -> a b (r d)", b=NB, r=RELS)
                with sp.Fori(0, BLKS) as i:
                    for j in range(BLK):
                        m = i * BLK + (NB * (t - 2) + j)
                        sp.wait_ge(xta_sb, m + 2)
                        sp.wait_ge(xtb_sb, m + 2)
                        sp.dma_start(tab[:, bass.ds(i * BLK + j, 1), :].rearrange("a o c -> a (o c)"),
                                     xt_out[:, j, :]).then_inc(xt_stored[j], 16)

            store_h(0)
            with sp.If(unsorted(sp) != 0):
                sp.wait_ge(record_free, K + 1)
                sp.dma_start(hit_w[:, :].bitcast(I32), sorted_d.rearrange("(p k) c -> p (k c)", k=K)).then_inc(records_in, 16)
                sp.dma_start(prev_last[1:P, :],
                             sorted_d[0:(P - 1) * K, :].rearrange("(p k) c -> p (k c)", k=K)[:, (K - 1) * REC:(K - 1) * REC + 1],
                             allow_slow_non_contiguous=True).then_inc(records_in, 16)
                sp.wait_ge(edges_sorted, 1)
            store_runs(0, 0, TURNS // 2)
            sp.wait_ge(bounds_ready, 1)
            sp.dma_start(end_d.rearrange("(h l) -> h l", l=LO), cum[:, :]).then_inc(bounds_out, 16)
            sp.dma_start(start_d.rearrange("(h l) -> h l", l=LO), hist_tmp[:, :]).then_inc(bounds_out, 16)
            sp.dma_start(end_idx_d.rearrange("(h l) -> h l", l=LO), hist_idx[:, :]).then_inc(bounds_out, 16)
            sp.wait_ge(bounds_out, 48)
            sp.dma_start(end_idx[:, :], end_idx_d[0:NODES].rearrange("(a b) -> a b", b=NB)).then_inc(idx_in, 16)
            for tile, d in ((end_b, end_d), (start_b, start_d)):
                sp.dma_start(tile, d[0:NODES].rearrange("(o n) -> o n", o=1).broadcast_to([P, NODES])).then_inc(bounds_in, 16)
            store_runs(0, TURNS // 2, TURNS)
            store_h(1)
            store_runs(1)
            store_xt(2)
            store_runs(2)
            store_xt(3)
            store_runs(3)
            o = out.rearrange("(a b) d -> a b d", b=NB)
            with sp.Fori(0, BLKS) as i:
                sp.wait_ge(res_ready, i + 1)
                sp.dma_start(o[:, bass.ds(i * BLK, BLK), :], res[:, :, :]).then_inc(res_out, 16)
            sp.wait_ge(res_out, 16 * BLKS + 1)
            for t in range(2):
                sp.wait_ge(table_out[t], 16 * BLKS + 1)
            sp.wait_ge(zero_out, 64)
            for s in range(SLOTS):
                sp.wait_ge(stored[s], 16 * len(SUBS) * TURNS * 4 + 1)
            for j in range(BLK):
                sp.wait_ge(xt_stored[j], 16 * BLKS * 2 + 1)

        @block.gpsimd
        def _(pool):
            made = Steps()

            def const(instruction):
                instruction.then_inc(consts_ready, 1)
                pool.wait_ge(consts_ready, made.next())

            const(pool.memset(dst_t[96:P, :], float(NODES)))
            const(pool.memset(src_t[96:P, :], 0.0))
            const(pool.memset(typ_t[96:P, :], 0.0))
            const(pool.memset(prev_last[:, :], -1.0))
            const(pool.memset(zero_row[:, :], 0.0))
            assert made.here == EDGE_CONSTS
            const(pool.memset(eps_c[:, :], LN_EPS))
            const(pool.memset(ones[:, :], 1.0))
            const(pool.affine_select(out=ident[:, :], in_=ones[:, :], compare_op=ALU.is_equal, fill=0.0, base=0,
                                     pattern=[[-1, P]], channel_multiplier=1))
            const(pool.affine_select(out=upper[:, :], in_=ones[0:HI, 0:HI], compare_op=ALU.is_gt, fill=0.0, base=0,
                                     pattern=[[1, HI]], channel_multiplier=-1))
            const(pool.iota(iota_f[:, :], pattern=[[1, LO]], base=0, channel_multiplier=0,
                            allow_small_or_imprecise_dtypes=True))
            const(pool.iota(lo_edge[:, :], pattern=[[0, 1]], base=0, channel_multiplier=K,
                            allow_small_or_imprecise_dtypes=True))
            const(pool.iota(hi_edge[:, :], pattern=[[0, 1]], base=K, channel_multiplier=K,
                            allow_small_or_imprecise_dtypes=True))
            const(pool.affine_select(out=before_w[:, :], in_=ones[:, :], compare_op=ALU.is_gt, fill=0.0, base=0,
                                     pattern=[[1, P]], channel_multiplier=-1))
            const(pool.affine_select(out=after_w[:, :], in_=ones[:, :], compare_op=ALU.is_ge, fill=0.0, base=0,
                                     pattern=[[-1, P]], channel_multiplier=1))
            assert made.here == CONSTS

            def gather_runs(l):
                with pool.Fori(0, TURNS) as i:
                    for s in range(SLOTS):
                        g = i * SLOTS + s
                        pool.wait_ge(idx_staged, g + (SLOTS * TURNS * l + 1))
                        pool.wait_ge(stored[s], i * (16 * len(SUBS)) + (16 * len(SUBS) * TURNS * l + 1))
                        pool.wait_ge(scan_done, g * GROUP + (CREDIT + K * l - GROUP + SUBS[0][1]))
                        pool.sem_inc(group_begun, 1)
                        for q, (k0, kn) in enumerate(SUBS):
                            for k in range(k0, k0 + kn):
                                pool.indirect_dma_start(
                                    out=ring[:, s, k, :], out_offset=None, in_=table[l],
                                    in_offset=bass.IndirectOffsetOnAxis(ap=idx_ring[:, s, k:k + 1], axis=0),
                                ).then_inc(landed[s][q], 16)

            def gather_ends(l):
                for s in range(SLOTS):
                    pool.wait_ge(stored[s], 16 * len(SUBS) * TURNS * (l + 1) + 1)
                if l == 0:
                    pool.wait_ge(zero_out, 64)
                    pool.wait_ge(idx_in, 16)
                else:
                    pool.wait_ge(agg_ready, BLKS * l + 1)
                for b in range(NB):
                    i, j = b // BLK, b % BLK
                    if i:
                        pool.wait_ge(end_row[j], 16 * (BLKS * l + i))
                    pool.indirect_dma_start(
                        out=ends[:, b, :], out_offset=None, in_=run_rows[l],
                        in_offset=bass.IndirectOffsetOnAxis(ap=end_idx[:, b:b + 1], axis=0),
                    ).then_inc(end_row[j], 16)

            with pool.If(unsorted(pool) != 0):
                pool.iota(end_w[:, :], pattern=[[1, CLASSES]], base=0, channel_multiplier=0,
                          allow_small_or_imprecise_dtypes=True).then_inc(classes_ready, 1)
                with pool.Fori(0, K) as i:
                    pool.wait_ge(record_ready, i + 1)
                    pool.sem_inc(group_begun, 1)
                    pool.indirect_dma_start(
                        out=sorted_d, out_offset=bass.IndirectOffsetOnAxis(ap=pos[:, :], axis=0),
                        in_=record[:, :], in_offset=None).then_inc(record_out, 16)
                    pool.wait_ge(record_out, i * 16 + 16)
                    pool.sem_inc(record_free, 1)
                pool.wait_ge(edges_sorted, 1)
            for l in range(4):
                if l < 2:
                    pool.wait_ge(table_out[l], 16 * BLKS + 1)
                else:
                    for j in range(BLK):
                        pool.wait_ge(xt_stored[j], 16 * BLKS * (l - 1) + 1)
                gather_runs(l)
                gather_ends(l)

        @block.scalar
        def _(act):
            def stage_idx(l):
                with act.Fori(0, TURNS) as i:
                    for s in range(SLOTS):
                        g = i * SLOTS + s
                        act.wait_ge(scan_done, g * GROUP + (K * l + CREDIT - GROUP))
                        act.copy(idx_ring[:, s, :], run_idx(l)[:, bass.ds(g * GROUP, GROUP)]).then_inc(idx_staged, 1)

            def blocks(t):
                per, base = {0: (1, 0), 1: (1, BLKS), 2: (2, 2 * BLKS)}.get(t, (0, 0))

                def copy_products(before, tiles):
                    for j in tiles:
                        m = before * BLK + (NB * (t - 2) + j)
                        act.wait_ge(xt_stored[j], before * 16 + (16 * BLKS * (t - 2) + 1))
                        for half, (full, copied) in enumerate(((xta_full, xta_sb), (xtb_full, xtb_sb))):
                            act.wait_ge(full, m + 1)
                            act.copy(xt_out[:, j, half * 512:half * 512 + 512],
                                     ps[0:NA, 6 + half, :]).then_inc(copied, 1)

                def root(k, r, layer_norm):
                    act.wait_ge(sq_ready, k * per + (base + r + 1))
                    if layer_norm:
                        act.activation(st[:, 2, :], st[:, 1, :], ACT.Sqrt, bias=eps_c[:, :],
                                       scale=1.0 / D).then_inc(root_ready, 1)
                    else:
                        act.activation(st[:, 2, :], st[:, 1, :], ACT.Sqrt).then_inc(root_ready, 1)

                def turn(k, before):
                    products = t >= 2 and before is not None
                    if products:
                        copy_products(before, (0,))
                    if k is not None and t in (1, 2):
                        act.wait_ge(agg_t_full, k + (BLKS * (t - 1) + 1))
                        act.copy(agg_t[:, :, 0:NA], ps_t[:, :, 0:NA]).then_inc(agg_t_sb, 1)
                    if products:
                        copy_products(before, (1, 2))
                    if k is not None and t in (0, 1, 2):
                        root(k, 0, t == 0)
                    if products:
                        copy_products(before, (3,))
                    if k is not None and t == 2:
                        root(k, 1, True)
                    if products:
                        copy_products(before, (4,))
                    if k is not None:
                        act.wait_ge(h_t_full, k + (BLKS * t + 2))
                        act.copy(h_tr[:, :, 0:NA], ps_t[:, :, 0:NA]).then_inc(h_t_sb, 1)

                pipeline(act, turn)

            act.wait_ge(consts_ready, CONSTS)
            blocks(0)
            with act.If(unsorted(act) != 0):
                act.wait_ge(edges_sorted, 1)
            act.wait_ge(edges_in, 16 * 7)
            stage_idx(0)
            blocks(1)
            stage_idx(1)
            blocks(2)
            act.wait_ge(idx_ready, 1)
            stage_idx(2)
            blocks(3)
            stage_idx(3)

        @block.tensor
        def _(pe):
            def count_before():
                chunks = [(c, min(512, CLASSES - c)) for c in range(0, CLASSES, 512)]

                def add(weights, start):
                    for c, width in chunks:
                        mm = pe.matmul(ps_seen[:, c:c + width], weights[:, :], hot[:, c:c + width],
                                       start=start, stop=True, skip_group_check=True)
                    return mm

                pe.wait_ge(sort_begun, 1)
                add(before_w, True).then_inc(seen_cleared, 1)
                with pe.Fori(0, K) as i:
                    pe.wait_ge(hot_made, i + 1)
                    add(before_w, False).then_inc(ranked, 1)
                    pe.wait_ge(rank_read, i + 1)
                    add(after_w, False).then_inc(counted, 1)

            def hist_groups():
                with pe.Fori(0, TURNS) as i:
                    for s in range(SLOTS):
                        g = i * SLOTS + s
                        pe.wait_ge(hot_ready, g * 2 + 2)
                        pe.wait_ge(hist_added, g + 1)
                        for k in range(GROUP):
                            mm = pe.matmul(ps_hist, hot_hi[:, k, :], hot_lo[:, k, :],
                                           start=(k == 0), stop=(k == GROUP - 1))
                        mm.then_inc(hist_part, 1)
                pe.wait_ge(tot_ready, 1)
                pe.matmul(ps_small[0:HI, 0:1], upper[:, :], cum[:, LO - 1:LO],
                          start=True, stop=True).then_inc(base_ready, 1)

            def carries(l):
                pe.wait_ge(last_copied, l + 1)
                pe.transpose(ps_t[:, 0, :], last_rows[:, :], ident[:, :]).then_inc(last_t, 1)
                pe.wait_ge(carry_scanned, l + 1)
                pe.transpose(ps_t[:, 1, :], carry_t[:, :], ident[:, :]).then_inc(carry_back, 1)
                pe.wait_ge(carry_split, l + 1)

            def blocks(t):
                def self_product(before):
                    pe.wait_ge(h_t_sb, before + (BLKS * t + 1))
                    pe.wait_ge(self_sb, before + (BLKS * t + 1))
                    for j in range(BLK):
                        mm = pe.matmul(ps_o[0:NA, j, :], h_tr[:, j, 0:NA], w_self[t][:, :],
                                       start=True, stop=True)
                    mm.then_inc(self_full, 1)

                def products(before, tiles):
                    for j in tiles:
                        m = before * BLK + (NB * (t - 2) + j)
                        for half, (full, copied) in enumerate(((xta_full, xta_sb), (xtb_full, xtb_sb))):
                            pe.wait_ge(copied, m + 1)
                            pe.matmul(ps[0:NA, 6 + half, :], h_tr[:, j, 0:NA],
                                      w_rel[t][:, 4 * half:4 * half + 4, :].rearrange("d r e -> d (r e)"),
                                      start=True, stop=True).then_inc(full, 1)

                def turn(k, before):
                    pending = t in (2, 3) and before is not None
                    if k is not None and t >= 1:
                        n = k + (BLKS * (t - 1) + 1)
                        pe.wait_ge(agg_ready, n)
                        for j in range(BLK):
                            for part in range(3):
                                mm = pe.matmul(ps_c[0:NA, j, :],
                                               span[:, bass.ds(k * BLK + j, 1), :].rearrange("p o a -> p (o a)"),
                                               carry_parts[:, part, :], start=(part == 0), stop=(part == 2))
                        mm.then_inc(c_full, 1)
                    if before is not None and t < 4:
                        self_product(before)
                    if pending:
                        products(before, (0,))
                    if k is not None and t in (1, 2):
                        pe.wait_ge(agg_ready, n + 1)
                        for j in range(BLK):
                            mm = pe.transpose(ps_t[:, j, 0:NA], agg[:, j, :], ident[0:NA, 0:NA])
                        mm.then_inc(agg_t_full, 1)
                    if pending:
                        products(before, (1,))
                    if k is not None and t in (1, 2):
                        pe.wait_ge(agg_t_sb, n)
                        pe.wait_ge(self_sb, k + (BLKS * t + 1))
                        for j in range(BLK):
                            mm = pe.matmul(ps_o[0:NA, j, :], agg_t[:, j, 0:NA], w_l[t][:, :], start=True, stop=True)
                        mm.then_inc(prod_full, 1)
                    if pending:
                        products(before, (2, 3, 4))
                    if k is not None and t < 4:
                        pe.wait_ge(h_ready, k + (BLKS * t + 1))
                        for j in range(BLK):
                            mm = pe.transpose(ps_t[:, j, 0:NA], h_t[:, j, :], ident[0:NA, 0:NA])
                        mm.then_inc(h_t_full, 1)

                pipeline(pe, turn)

            pe.wait_ge(consts_ready, CONSTS)
            pe.wait_ge(weights_in, 16 * N_WEIGHTS)
            blocks(0)
            pe.wait_ge(unsorted_ready, 1)
            pe.matmul(ps_small[0:1, 0:1], ones[:, 0:1], unsorted_p[:, 0:1], start=True, stop=True).then_inc(check_sum, 1)
            with pe.If(unsorted(pe) != 0):
                count_before()
                pe.wait_ge(edges_sorted, 1)
            pe.wait_ge(passes_ready, 1)
            pe.matmul(ps_c[:, 0, :], passes_w[:, :], ident[:, :], start=True, stop=True).then_inc(passes_bc, 1)
            hist_groups()
            for t in range(1, 5):
                carries(t - 1)
                if t == 1:
                    pe.wait_ge(span_ready, 1)
                blocks(t)

        @block.vector
        def _(dve):
            v = Steps()

            def step(instruction):
                instruction.then_inc(vec, 1)
                dve.wait_ge(vec, v.next())

            def over(column):
                return column.unsqueeze(2).broadcast_to([NA, BLK, D])

            def blocks(t):
                op = ALU.max if t < 3 else ALU.add

                def turn(k, before):
                    roots = {0: (1, 0), 1: (1, BLKS), 2: (2, 2 * BLKS)}.get(t)
                    if k is not None:
                        tiles = bass.ds(k * BLK, BLK)
                        xs, selfs = x_all[:, tiles, :], self_all[:, tiles, :]
                    if k is not None and t >= 1:
                        n = k + (BLKS * (t - 1) + 1)
                        for j in range(BLK):
                            dve.wait_ge(end_row[j], k * 16 + 16 * (BLKS * (t - 1) + 1))
                        dve.wait_ge(c_full, n)
                        dve.tensor_tensor(agg[:, :, :], ends[:, tiles, :], ps_c[0:NA, :, :], op).then_inc(agg_ready, 1)
                    if t == 0 and k is not None:
                        dve.wait_ge(x_first_in if before is None else x_in, 16)
                    if before is not None and t < 4:
                        dve.wait_ge(weights_in, 16 * N_WEIGHTS)
                        dve.wait_ge(self_full, before + (BLKS * t + 1))
                        dve.tensor_tensor(self_all[:, bass.ds(before * BLK, BLK), :], ps_o[0:NA, :, :],
                                          b_self[t][:, :].unsqueeze(1).broadcast_to([NA, BLK, D]),
                                          ALU.add).then_inc(self_sb, 1)
                        dve.wait_ge(self_sb, before + (BLKS * t + 2))
                    if k is None:
                        return
                    if t in (1, 2):
                        dve.wait_ge(prod_full, n)
                        step(dve.tensor_tensor(o_t[:, :, :], ps_o[0:NA, :, :], selfs, ALU.add))
                        step(dve.tensor_tensor(sq_t[:, :, :], o_t[:, :, :], o_t[:, :, :], ALU.mult))
                        dve.tensor_reduce(st[:, 1, :], sq_t[:, :, :], AX.X, ALU.add).then_inc(sq_ready, 1)
                        dve.wait_ge(root_ready, k * roots[0] + (roots[1] + 1))
                        step(dve.tensor_scalar(st[:, 3, :], st[:, 2, :], NORM_EPS, None, ALU.max))
                        step(dve.reciprocal(st[:, 3, :], st[:, 3, :]))
                    if t == 2:
                        step(dve.scalar_tensor_tensor(out=o_t[:, :, :], in0=o_t[:, :, :], scalar=0.0,
                                                      in1=over(st[:, 3, :]), op0=ALU.max, op1=ALU.mult))
                        step(dve.tensor_tensor(o_t[:, :, :], xs, o_t[:, :, :], ALU.add))
                    if t in (0, 2):
                        y = xs if t == 0 else o_t[:, :, :]
                        step(dve.tensor_reduce(st[:, 0, :], y, AX.X, ALU.add))
                        step(dve.tensor_scalar(st[:, 0, :], st[:, 0, :], -1.0 / D, None, ALU.mult))
                        step(dve.tensor_tensor(cen[:, :, :], y, over(st[:, 0, :]), ALU.add))
                        step(dve.tensor_tensor(sq_t[:, :, :], cen[:, :, :], cen[:, :, :], ALU.mult))
                        dve.tensor_reduce(st[:, 1, :], sq_t[:, :, :], AX.X, ALU.add).then_inc(sq_ready, 1)
                        dve.wait_ge(root_ready, k * roots[0] + (roots[1] + roots[0]))
                        step(dve.reciprocal(st[:, 3, :], st[:, 2, :]))
                    if t in (3, 4):
                        dve.wait_ge(agg_ready, n + 1)
                        step(dve.tensor_tensor(o_t[:, :, :], agg[:, :, :], selfs, ALU.add))
                    if t < 4:
                        dve.wait_ge(h_t_full, k + (BLKS * t + 1))
                        if t < 2:
                            dve.wait_ge(table_out[t], k * 16 + 1)
                        if t == 3:
                            dve.tensor_scalar(h_t[:, :, :], o_t[:, :, :], 0.0, None, ALU.max).then_inc(h_ready, 1)
                        else:
                            raw = o_t if t == 1 else cen
                            dve.scalar_tensor_tensor(out=h_t[:, :, :], in0=raw[:, :, :], scalar=0.0,
                                                     in1=over(st[:, 3, :]), op0=ALU.max,
                                                     op1=ALU.mult).then_inc(h_ready, 1)
                        if t == 2:
                            step(dve.tensor_copy(xs, o_t[:, :, :]))
                    if t == 4:
                        dve.wait_ge(res_out, k * 16 + 1)
                        dve.scalar_tensor_tensor(out=res[:, :, :], in0=o_t[:, :, :], scalar=0.0, in1=xs,
                                                 op0=ALU.max, op1=ALU.add).then_inc(res_ready, 1)

                pipeline(dve, turn, v, {0: 5, 1: 4, 2: 12, 3: 1, 4: 1}[t])

            def one_hots(g):
                dve.wait_ge(hist_part, g + 1)
                for hot, part, n in ((hot_hi, dst_hi, HI), (hot_lo, dst_lo, LO)):
                    dve.tensor_tensor(hot[:, :, :],
                                      part[:, bass.ds(g * GROUP, GROUP)].unsqueeze(2).broadcast_to([P, GROUP, n]),
                                      iota_f[:, 0:n].unsqueeze(1).broadcast_to([P, GROUP, n]),
                                      ALU.is_equal).then_inc(hot_ready, 1)

            def scan_group(l, i, s):
                g = i * SLOTS + s
                for q, (k0, kn) in enumerate(SUBS):
                    dve.wait_ge(landed[s][q], i * (16 * kn) + 16 * kn * (TURNS * l + 1))
                    for k in range(k0, k0 + kn):
                        before = ring[:, s, k - 1, :] if k else ring[:, 1 - s, GROUP - 1, :]
                        at = g * GROUP + k
                        dve.wait_ge(scan_done, at + (CREDIT + K * l))
                        dve.scalar_tensor_tensor(out=ring[:, s, k, :], in0=before,
                                                 scalar=same[:, bass.ds(at, 1)], in1=ring[:, s, k, :],
                                                 op0=ALU.mult, op1=ALU.max if l < 2 else ALU.add).then_inc(scan_done, 1)

            def scan_runs(l, first, last):
                with dve.Fori(first, last) as i:
                    for s in range(SLOTS):
                        scan_group(l, i, s)

            def keep_last(l):
                dve.wait_ge(scan_done, CREDIT + K * (l + 1))
                dve.tensor_copy(last_rows[:, :], ring[:, SLOTS - 1, GROUP - 1, :]).then_inc(last_copied, 1)

            def count_groups(g):
                for c in (g * 2, g * 2 + 1):
                    one_hots(c)
                    dve.wait_ge(hist_part, c + 2)
                    dve.tensor_tensor(hist[:, :], hist[:, :], ps_hist, ALU.add).then_inc(hist_added, 1)
                    dve.wait_ge(hist_added, c + 2)

            def scan_first_layer():
                half = TURNS // 2
                assert TURNS == 2 * half + 1 and SLOTS == 2
                with dve.Fori(0, half) as i:
                    for s in range(SLOTS):
                        count_groups(i * SLOTS + s)
                        scan_group(0, i, s)
                count_groups(half * SLOTS)
                node_bounds()
                scan_group(0, half, 0)
                scan_group(0, half, 1)
                spans()
                scan_runs(0, half + 1, TURNS)

            def node_bounds():
                step(dve.tensor_tensor_scan(cum[:, :], ones[0:HI, 0:LO], hist[:, :], 0.0, ALU.mult, ALU.add))
                dve.sem_inc(tot_ready, 1)
                dve.wait_ge(base_ready, 1)
                step(dve.tensor_copy(hist_base[:, :], ps_small[0:HI, 0:1]))
                step(dve.tensor_scalar(cum[:, :], cum[:, :], hist_base[:, :], -1.0, ALU.add, ALU.add))
                step(dve.scalar_tensor_tensor(out=hist_tmp[:, :], in0=cum[:, :], scalar=1.0, in1=hist[:, :],
                                              op0=ALU.add, op1=ALU.subtract))
                step(dve.tensor_scalar(hist_new[:, :], cum[:, :], -1.0, float(EMPTY_ROW), ALU.mult, ALU.add))
                step(dve.scalar_tensor_tensor(out=hist_new[:, :], in0=hist[:, :], scalar=0.0, in1=hist_new[:, :],
                                              op0=ALU.is_equal, op1=ALU.mult))
                dve.tensor_tensor(hist_idx[:, :], hist_new[:, :], cum[:, :], ALU.add).then_inc(bounds_ready, 1)

            def spans():
                dve.wait_ge(bounds_in, 32)
                step(dve.tensor_scalar(hit, end_b, hi_edge[:, :], None, ALU.is_lt))
                step(dve.scalar_tensor_tensor(out=hit, in0=end_b, scalar=lo_edge[:, :], in1=hit,
                                              op0=ALU.is_ge, op1=ALU.mult))
                dve.scalar_tensor_tensor(out=span[:, :, :].rearrange("p b a -> p a b"),
                                         in0=start_b.rearrange("p (a b) -> p a b", b=NB),
                                         scalar=lo_edge[:, :],
                                         in1=hit.rearrange("p (a b) -> p a b", b=NB),
                                         op0=ALU.is_lt, op1=ALU.mult).then_inc(span_ready, 1)

            def carries(l):
                dve.wait_ge(last_t, l + 1)
                dve.tensor_tensor_scan(carry_t[:, 1:P], passes_b[:, 0:P - 1], ps_t[:, 0, 0:P - 1], 0.0,
                                       ALU.mult, ALU.max if l < 2 else ALU.add).then_inc(carry_scanned, 1)
                dve.wait_ge(carry_back, l + 1)
                step(dve.tensor_copy(carry_parts[:, 0, :], ps_t[:, 1, :]))
                step(dve.tensor_tensor(carry[:, :], ps_t[:, 1, :], carry_parts[:, 0, :], ALU.subtract))
                step(dve.tensor_copy(carry_parts[:, 1, :], carry[:, :]))
                step(dve.tensor_tensor(carry_r[:, :], carry[:, :], carry_parts[:, 1, :], ALU.subtract))
                dve.tensor_copy(carry_parts[:, 2, :], carry_r[:, :]).then_inc(carry_split, 1)

            def sort_edges():
                w = Steps()

                def sort_step(instruction):
                    instruction.then_inc(sort_vec, 1)
                    dve.wait_ge(sort_vec, w.next())

                dve.memset(hot[:, :], 0.0).then_inc(sort_begun, 1)
                sort_step(dve.tensor_copy(dst_f[:, :], dst_t[:, :]))
                dve.wait_ge(seen_cleared, 1)
                dve.wait_ge(classes_ready, 1)
                with dve.Fori(0, K) as i:
                    w.loop(i, 3)
                    dve.wait_ge(counted, i + 1)
                    dve.tensor_scalar(hot[:, :], end_w[:, :], dst_f[:, bass.ds(i, 1)], None,
                                      ALU.is_equal).then_inc(hot_made, 1)
                    dve.wait_ge(hot_made, i + 1)
                    dve.wait_ge(ranked, i + 1)
                    sort_step(dve.tensor_tensor(hit_w[:, 0:CLASSES], ps_seen, hot[:, :], ALU.mult))
                    sort_step(dve.tensor_reduce(col[:, :], hit_w[:, 0:CLASSES], AX.X, ALU.add))
                    sort_step(dve.tensor_scalar(rank[:, bass.ds(i, 1)], col[:, :], 0.0, None, ALU.add))
                    dve.sem_inc(rank_read, 1)
                w.end_loop(K)
                dve.wait_ge(counted, K + 1)
                sort_step(dve.memset(hit_w[:, 0:CLASSES], 1.0))
                sort_step(dve.tensor_tensor_scan(start_w[:, :], hit_w[:, 0:CLASSES], ps_seen, 0.0, ALU.mult, ALU.add))
                sort_step(dve.tensor_tensor(start_w[:, :], start_w[:, :], ps_seen, ALU.subtract))
                with dve.Fori(0, K) as i:
                    w.loop(i, 6)
                    sort_step(dve.scalar_tensor_tensor(out=hit_w[:, 0:CLASSES], in0=end_w[:, :],
                                                  scalar=dst_f[:, bass.ds(i, 1)], in1=start_w[:, :],
                                                  op0=ALU.is_equal, op1=ALU.mult))
                    sort_step(dve.tensor_reduce(col[:, :], hit_w[:, 0:CLASSES], AX.X, ALU.add))
                    dve.wait_ge(record_free, i + 1)
                    sort_step(dve.tensor_scalar(pos[:, :], rank[:, bass.ds(i, 1)], col[:, :], None, ALU.add))
                    for c, tile in enumerate((dst_t, src_t, typ_t)):
                        sort_step(dve.tensor_scalar(record[:, c:c + 1], tile[:, bass.ds(i, 1)], 0.0, None, ALU.add))
                    dve.sem_inc(record_ready, 1)
                w.end_loop(K)
                dve.wait_ge(records_in, 32)
                for c, tile in enumerate((dst_t, src_t, typ_t)):
                    sort_step(dve.tensor_copy(tile[:, :], hit_w[:, :].bitcast(I32).rearrange("p (k c) -> p k c", c=REC)[:, :, c]))
                dve.sem_inc(edges_sorted, 1)

            for free in (agg_ready, xta_sb, xtb_sb, h_t_full, table_out[0], table_out[1], res_out, hist_part,
                         hist_added, counted, record_free, self_sb, *stored, *xt_stored):
                dve.sem_inc(free, 1)
            dve.sem_inc(scan_done, CREDIT)
            step(dve.memset(ring[:, SLOTS - 1, GROUP - 1, :], 0.0))
            step(dve.memset(hist[:, :], 0.0))
            step(dve.memset(carry_t[:, 0:1], 0.0))
            step(dve.memset(same[:, 0:1], 0.0))
            step(dve.memset(record[:, :], 0))

            blocks(0)

            dve.wait_ge(consts_ready, CONSTS)
            dve.wait_ge(edges_in, 16 * 7)
            step(dve.tensor_tensor(scr1[:, 0:K - 1], dst_t[:, 1:K], dst_t[:, 0:K - 1], ALU.is_lt))
            step(dve.tensor_reduce(unsorted_p[:, 0:1], scr1[:, 0:K - 1], AX.X, ALU.add))
            step(dve.tensor_tensor(unsorted_p[:, 1:2], dst_t[:, 0:1], prev_last[:, :], ALU.is_lt))
            dve.tensor_tensor(unsorted_p[:, 0:1], unsorted_p[:, 0:1], unsorted_p[:, 1:2], ALU.add).then_inc(unsorted_ready, 1)
            dve.wait_ge(check_sum, 1)
            dve.tensor_copy(unsorted_i[:, :], ps_small[0:1, 0:1]).then_inc(check_int, 1)

            with dve.If(unsorted(dve) != 0):
                sort_edges()
            step(dve.tensor_tensor(same[:, 1:K], dst_t[:, 1:K], dst_t[:, 0:K - 1], ALU.is_equal))
            step(dve.tensor_scalar(dst_hi[:, :], dst_t[:, :], 6, None, ALU.logical_shift_right))
            step(dve.tensor_scalar(dst_lo[:, :], dst_t[:, :], LO - 1, None, ALU.bitwise_and))
            dve.scalar_tensor_tensor(out=rel_idx[:, :], in0=src_t[:, :], scalar=float(RELS), in1=typ_t[:, :],
                                     op0=ALU.mult, op1=ALU.add).then_inc(idx_ready, 1)
            step(dve.tensor_tensor(passes[:, :], dst_t[:, 0:1], prev_last[:, :], ALU.is_equal))
            step(dve.tensor_copy(passes_last[:, :], dst_t[:, K - 1:K]))
            step(dve.scalar_tensor_tensor(out=passes[:, :], in0=dst_t[:, 0:1], scalar=passes_last[:, :],
                                          in1=passes[:, :], op0=ALU.is_equal, op1=ALU.mult))
            dve.tensor_scalar(passes_w[:, :], ones[:, :], passes[:, :], None, ALU.mult).then_inc(passes_ready, 1)
            dve.wait_ge(passes_bc, 1)
            step(dve.tensor_copy(passes_b[:, :], ps_c[:, 0, :]))
            for l in range(4):
                if l == 0:
                    scan_first_layer()
                else:
                    scan_runs(l, 0, TURNS)
                keep_last(l)
                carries(l)
                blocks(l + 1)


INPUTS = ["x", "src", "dst", "edge_type_8", "L0_gnn_W_l1", "L0_gnn_W_r1", "L0_gnn_b1", "L0_gnn_W_l2", "L0_gnn_W_r2",
          "L0_gnn_b2", "L1_gnn_w1", "L1_gnn_sl1", "L1_gnn_b1", "L1_gnn_w2", "L1_gnn_sl2", "L1_gnn_b2"]


def kernel(**inputs):
    import numpy as np
    import concourse.bacc as bacc
    from concourse.bass_utils import run_bass_kernel_spmd

    nc = bacc.Bacc("TRN2", target_bir_lowering=False, num_devices=1)
    arrays, args = {}, []
    for name in INPUTS:
        a = np.ascontiguousarray(inputs[name])
        arrays[f"in_{name}"] = a
        args.append(nc.dram_tensor(f"in_{name}", a.shape, mybir.dt.from_np(a.dtype), kind="ExternalInput").ap())
    out = nc.dram_tensor("out", (NODES, D), F32, kind="ExternalOutput").ap()
    build(nc, *args, out)
    return run_bass_kernel_spmd(nc, [arrays], core_ids=[0]).results[0]["out"]
```

```python
from contextlib import ExitStack

import concourse.bass as bass
from concourse import mybir

F32 = mybir.dt.float32
BF16 = mybir.dt.bfloat16
I32 = mybir.dt.int32
ALU = mybir.AluOpType
ACT = mybir.ActivationFunctionType
AX = mybir.AxisListType

P = 128
D = 128
NODES = 3125
NA, NB = 125, 25
EDGES = 103125
K = -(-EDGES // P)
TAIL = EDGES - (P - 1) * K
RELS = 8
GROUP = 31
SLOTS = 2
TURNS = K // (GROUP * SLOTS)
PE_STEPS = 5
BANK_STEPS = 4
PE_FIRST = GROUP - PE_STEPS
LANDS = {"max": [(0, 5), (5, 5), (10, 5), (15, 5), (20, 6)], "sum": [(0, 8), (8, 8), (16, 8), (24, 7)]}
STORES = {"max": [(0, 8), (8, 9), (17, 9), (26, 5)], "sum": [(0, 8), (8, 8), (16, 8), (24, 7)]}
KIND = ["max", "max", "sum", "sum"]
GROUPS = K // GROUP
HALF = TURNS // 2
PIECE = NODES // (TURNS - 2 - HALF)
BLK = 5
BLKS = NB // BLK
HI, LO = 49, 64
CLASSES = NODES + 1
REC = 4
EMPTY_ROW = P * K
LN_EPS = 1e-5
NORM_EPS = 1e-12
CREDIT = SLOTS * GROUP
SPLIT = ((0, 112), (112, NA))
N_STORES = 4
EDGE_CONSTS, CONSTS = 5, 16
N_WEIGHTS = 4 * 2 + 2 + 2
assert K == GROUP * SLOTS * TURNS and NA * NB == NODES and GROUPS == TURNS * SLOTS and TURNS == 2 * HALF + 1
assert PIECE * (TURNS - 2 - HALF) == NODES


class Steps:

    def __init__(self):
        self.base, self.here, self.i, self.per = 0, 0, None, 0

    def loop(self, i, per):
        self.base, self.here, self.i, self.per = self.base + self.here, 0, i, per

    def end_loop(self, turns):
        assert self.here == self.per, (self.here, self.per)
        self.base, self.here, self.i = self.base + turns * self.per, 0, None

    def next(self):
        self.here += 1
        return self.base + self.here if self.i is None else self.i * self.per + (self.base + self.here)


def build(nc, x, src, dst, edge_type_8, W_l1, W_r1, sb1, W_l2, W_r2, sb2, w1, sl1, rb1, w2, sl2, rb2, out):
    with ExitStack() as ctx:
        def sb(name, shape, dt=F32):
            return ctx.enter_context(nc.sbuf_tensor(name, shape, dt))

        def sem(name):
            return ctx.enter_context(nc.semaphore(name))

        def scratch(name, shape, dt=F32):
            return nc.dram_tensor(name, shape, dt).ap()

        table = [scratch("table0", (NODES, D)), scratch("table1", (NODES, D)),
                 scratch("table2", (NODES * RELS, D)), scratch("table3", (NODES * RELS, D))]
        sorted_d = scratch("sorted_d", (P * K, REC), I32)
        run_rows = [scratch(f"run_rows{l}", (P * K + 1, D)) for l in range(4)]
        end_d, start_d, end_idx_d = scratch("end_d", (HI * LO,)), scratch("start_d", (HI * LO,)), \
            scratch("end_idx_d", (HI * LO,), I32)

        src_t = sb("src_t", [P, K], I32)
        dst_t = sb("dst_t", [P, K], I32)
        typ_t = sb("typ_t", [P, K], I32)
        prev_last = sb("prev_last", [P, 1], I32)
        dst_hi = sb("dst_hi", [P, K], BF16)
        dst_lo = sb("dst_lo", [P, K], BF16)
        rel_idx = sb("rel_idx", [P, K], I32)
        same = typ_t[:, :].bitcast(F32)
        idx_ring = sb("idx_ring", [P, SLOTS, GROUP], I32)
        ring = sb("ring", [P, SLOTS, GROUP, D])
        spare = ring[:, 0, :, :].rearrange("p k d -> p (k d)")
        dst_f = spare[:, 0:K]
        rank = spare[:, K:2 * K]
        hot = spare[:, 2 * K:2 * K + CLASSES // 2].bitcast(BF16)
        x_all = sb("x_all", [NA, NB, D])
        self_all = sb("self_all", [NA, NB, D])
        ends = sb("ends", [NA, NB, D])
        end_idx = sb("end_idx", [NA, NB], I32)
        span = sb("span", [P, NB, NA], BF16)
        end_w = sb("end_w", [P, NB * D])
        start_w = sb("start_w", [P, CLASSES])
        h_all = end_w[0:NA, :].rearrange("p (b d) -> p b d", b=NB)
        hit_w = sb("hit_w", [P, K * REC])
        end_b, start_b, hit = end_w[:, 0:NODES], start_w[:, 0:NODES], hit_w[:, 0:NODES]
        dst_part = hit_w[:, 0:K].bitcast(I32)
        before_w = sb("before_w", [P, P], BF16)
        after_w = sb("after_w", [P, P], BF16)
        col = sb("col", [P, 1])
        pos = sb("pos", [P, 1], I32)
        record = sb("record", [P, REC], I32)
        hot_hi = sb("hot_hi", [P, HI, GROUP], BF16)
        hot_lo = sb("hot_lo", [P, LO, GROUP], BF16)
        class_no = sb("class_no", [P, LO, GROUP], BF16)
        lo_edge = sb("lo_edge", [P, 1])
        hi_edge = sb("hi_edge", [P, 1])
        ident = sb("ident", [P, P])
        ones = sb("ones", [P, P])
        upper = sb("upper", [HI, HI])
        hist = sb("hist", [HI, LO])
        cum = sb("cum", [HI, LO])
        hist_tmp = sb("hist_tmp", [HI, LO])
        hist_new = sb("hist_new", [HI, LO])
        hist_idx = sb("hist_idx", [HI, LO], I32)
        hist_base = sb("hist_base", [HI, 1])
        zero_row = sb("zero_row", [1, D])
        passes = sb("passes", [P, 1])
        passes_last = sb("passes_last", [P, 1])
        passes_w = sb("passes_w", [P, P])
        passes_b = sb("passes_b", [P, P])
        unsorted_p = sb("unsorted_p", [P, 2])
        unsorted_i = sb("unsorted_i", [1, 1], I32)
        carry_t = sb("carry_t", [P, P])
        carry = sb("carry", [P, D])
        carry_r = sb("carry_r", [P, D])
        carry_parts = sb("carry_parts", [P, 3, D], BF16)
        last_rows = sb("last_rows", [P, D])
        agg = sb("agg", [NA, BLK, D])
        agg_t = sb("agg_t", [P, BLK, P])
        o_t = sb("o_t", [NA, BLK, D])
        sq_t = sb("sq_t", [NA, BLK, D])
        cen = sb("cen", [NA, BLK, D])
        h_t = sb("h_t", [NA, BLK, D])
        h_tr = sb("h_tr", [P, BLK, P])
        res = cen
        st = sb("st", [NA, 4, BLK])
        xt_out = sb("xt_out", [NA, BLK, RELS * D])
        h_parts = xt_out[:, :, :].rearrange("p j c -> p (j c)").bitcast(BF16)[:, 0:NB * 3 * D] \
            .rearrange("p (b c d) -> p b c d", b=NB, c=3)
        src_hot = ends[:, :, :].rearrange("p b d -> p (b d)").bitcast(BF16) \
            .rearrange("p (o b e) -> p o b e", o=2, b=NB)
        tile_no = sb("tile_no", [NA, NB, P], BF16)
        lane_base = sb("lane_base", [NA, 1])
        src_off = sb("src_off", [NA, PE_STEPS, P], BF16)
        src_cols = sb("src_cols", [P, SLOTS, PE_STEPS])
        eps_c = sb("eps_c", [NA, 1])
        w_l = [None, sb("w_l1", [D, D]), sb("w_l2", [D, D])]
        w_self = [sb(f"w_self{t}", [D, D]) for t in range(4)]
        b_self = [sb(f"b_self{t}", [NA, D]) for t in range(4)]
        w_rel = [None, None, sb("w_rel2", [D, RELS, D]), sb("w_rel3", [D, RELS, D])]

        ps = ctx.enter_context(nc.psum_tensor("ps", [P, 8, 512], F32))
        flat = ps[:, :, :].rearrange("p b n -> p (b n)")
        ps_c = flat[:, 0:BLK * P].rearrange("p (j n) -> p j n", n=P)
        ps_t = flat[:, 1024:1024 + BLK * P].rearrange("p (j n) -> p j n", n=P)
        ps_o = flat[:, 2048:2048 + BLK * P].rearrange("p (j n) -> p j n", n=P)
        ps_xa, ps_xb = ps[:, 6, :], ps[:, 7, :]
        ps_rows = [flat[:, 1024 * s:1024 * s + PE_STEPS * P].rearrange("p (m d) -> p m d", m=PE_STEPS)
                   for s in range(SLOTS)]
        ps_src = flat[0:NA, 2048:2048 + PE_STEPS * P].rearrange("p (m e) -> p m e", m=PE_STEPS)
        ps_passes = ps[:, 6, 0:P]
        ps_hist = ps[0:HI, 6, 0:LO]
        ps_seen = flat[:, 0:CLASSES]
        ps_small = ps[:, 7, 0:8]

        edges_in = sem("edges_in")
        x_first_in = sem("x_first_in")
        x_in = sem("x_in")
        weights_in = sem("weights_in")
        consts_ready = sem("consts_ready")
        vec = sem("vec")
        unsorted_ready = sem("unsorted_ready")
        check_sum = sem("check_sum")
        check_int = sem("check_int")
        sort_vec = sem("sort_vec")
        sort_begun = sem("sort_begun")
        classes_ready = sem("classes_ready")
        seen_cleared = sem("seen_cleared")
        hot_made = sem("hot_made")
        ranked = sem("ranked")
        rank_read = sem("rank_read")
        counted = sem("counted")
        record_ready = sem("record_ready")
        record_out = sem("record_out")
        record_free = sem("record_free")
        records_in = sem("records_in")
        edges_sorted = sem("edges_sorted")
        idx_ready = sem("idx_ready")
        idx_staged = sem("idx_staged")
        group_begun = sem("group_begun")
        landed = {kind: [[sem(f"landed_{kind}{s}{q}") for q in range(len(parts))] for s in range(SLOTS)]
                  for kind, parts in LANDS.items()}
        part0, part1, part2 = sem("part0"), sem("part1"), sem("part2")
        rest_ready = sem("rest_ready")
        src_staged = sem("src_staged")
        src_spread = sem("src_spread")
        off_ready = sem("off_ready")
        src_hot_made = sem("src_hot_made")
        rows_fetched = sem("rows_fetched")
        scan_done = sem("scan_done")
        stored = [sem(f"stored{s}") for s in range(SLOTS)]
        hot_ready = sem("hot_ready")
        hist_part = sem("hist_part")
        hist_added = sem("hist_added")
        base_ready = sem("base_ready")
        tot_ready = sem("tot_ready")
        bounds_ready = sem("bounds_ready")
        bounds_out = sem("bounds_out")
        bounds_in = sem("bounds_in")
        idx_in = sem("idx_in")
        span_ready = sem("span_ready")
        passes_ready = sem("passes_ready")
        passes_bc = sem("passes_bc")
        last_copied = sem("last_copied")
        last_t = sem("last_t")
        carry_scanned = sem("carry_scanned")
        carry_back = sem("carry_back")
        carry_split = sem("carry_split")
        end_row = [sem(f"end_row{j}") for j in range(BLK)]
        zero_out = sem("zero_out")
        c_full = sem("c_full")
        agg_ready = sem("agg_ready")
        agg_t_full = sem("agg_t_full")
        agg_t_sb = sem("agg_t_sb")
        prod_full = sem("prod_full")
        prod_read = sem("prod_read")
        sq_ready = sem("sq_ready")
        root_ready = sem("root_ready")
        x_added = sem("x_added")
        h_ready = sem("h_ready")
        h_kept = sem("h_kept")
        h_t_full = sem("h_t_full")
        h_t_sb = sem("h_t_sb")
        self_full = sem("self_full")
        self_sb = sem("self_sb")
        xta_full, xta_sb = sem("xta_full"), sem("xta_sb")
        xtb_full, xtb_sb = sem("xtb_full"), sem("xtb_sb")
        xt_stored = [sem(f"xt_stored{j}") for j in range(BLK)]
        table_out = [sem(f"table_out{t}") for t in range(2)]
        res_ready = sem("res_ready")
        res_out = sem("res_out")

        def run_idx(l):
            return src_t if l < 2 else rel_idx

        def pipeline(eng, turn, steps=None, per=0):
            turn(None, None, 0)
            turn(None, 0, 1)
            with eng.Fori(0, BLKS - 2) as u:
                if steps:
                    steps.loop(u, per)
                turn(u, u + 1, u + 2)
                if steps:
                    steps.end_loop(BLKS - 2)
            turn(BLKS - 2, BLKS - 1, None)
            turn(BLKS - 1, None, None)

        def unsorted(eng):
            eng.wait_ge(check_int, 1)
            return eng.value_load(unsorted_i[:, :], min_val=0, max_val=P * K)

        block = ctx.enter_context(nc.Block())

        @block.sync
        def _(sp):
            x_tiles = x.rearrange("(a b) d -> a b d", b=NB)
            for a, z in SPLIT:
                sp.dma_start(x_all[a:z, 0:BLK, :], x_tiles[a:z, 0:BLK, :]).then_inc(x_first_in, 16)
            for a, z in SPLIT:
                sp.dma_start(x_all[a:z, BLK:NB, :], x_tiles[a:z, BLK:NB, :]).then_inc(x_in, 16)
            sp.wait_ge(consts_ready, EDGE_CONSTS)
            for tile, d in ((dst_t, dst), (src_t, src), (typ_t, edge_type_8)):
                for a, z in ((0, 112), (112, P - 1)):
                    sp.dma_start(tile[a:z, :], d[a * K:z * K].rearrange("(p k) -> p k", k=K)).then_inc(edges_in, 16)
                sp.dma_start(tile[P - 1:P, 0:TAIL], d[(P - 1) * K:EDGES].rearrange("(p k) -> p k", p=1)).then_inc(edges_in, 16)
            sp.dma_start(prev_last[1:P, :], dst[0:(P - 1) * K].rearrange("(p k) -> p k", k=K)[:, K - 1:K],
                         allow_slow_non_contiguous=True).then_inc(edges_in, 16)
            for t, (w, b) in enumerate(((W_r1, sb1), (W_r2, sb2), (sl1, rb1), (sl2, rb2))):
                sp.dma_start(w_self[t][:, :], w).then_inc(weights_in, 16)
                sp.dma_start(b_self[t][:, :], b.rearrange("(o d) -> o d", o=1).broadcast_to([NA, D])).then_inc(weights_in, 16)
            for t, w in ((1, W_l1), (2, W_l2)):
                sp.dma_start(w_l[t][:, :], w).then_inc(weights_in, 16)
            for t, w in ((2, w1), (3, w2)):
                sp.dma_start(w_rel[t][:, :, :], w.rearrange("r d e -> d r e")).then_inc(weights_in, 16)
            for l in range(4):
                sp.dma_start(run_rows[l][EMPTY_ROW:EMPTY_ROW + 1, :], zero_row[:, :]).then_inc(zero_out, 16)

            def store_h(t):
                tab = table[t].rearrange("(a b) d -> a b d", b=NB)
                with sp.Fori(0, BLKS) as i:
                    sp.wait_ge(h_ready, i + (BLKS * t + 1))
                    for a, z in SPLIT:
                        sp.dma_start(tab[a:z, bass.ds(i * BLK, BLK), :], h_t[a:z, :, :]).then_inc(table_out[t], 16)

            def store_group(l, i, s):
                rows = run_rows[l][0:P * K, :].rearrange("(p k) d -> p k d", k=K)
                for k0, kn in STORES[KIND[l]]:
                    at = s * GROUP + k0
                    sp.wait_ge(scan_done, i * (SLOTS * GROUP) + (CREDIT + K * l + at + kn))
                    sp.dma_start(rows[:, bass.ds(i * (SLOTS * GROUP) + at, kn), :],
                                 ring[:, s, k0:k0 + kn, :]).then_inc(stored[s], 16)

            def store_runs(l, first=0, last=TURNS):
                with sp.Fori(first, last) as i:
                    for s in range(SLOTS):
                        store_group(l, i, s)

            def store_xt(t):
                tab = table[t].rearrange("(a b r) d -> a b (r d)", b=NB, r=RELS)
                with sp.Fori(0, BLKS) as i:
                    for j in range(BLK):
                        m = i * BLK + (NB * (t - 2) + j)
                        sp.wait_ge(xta_sb, m + 2)
                        sp.wait_ge(xtb_sb, m + 2)
                        for a, z in SPLIT:
                            sp.dma_start(tab[a:z, bass.ds(i * BLK + j, 1), :].rearrange("a o c -> a (o c)"),
                                         xt_out[a:z, j, :]).then_inc(xt_stored[j], 16)

            store_h(0)
            with sp.If(unsorted(sp) != 0):
                sp.wait_ge(record_free, K + 1)
                sp.dma_start(hit_w[:, :].bitcast(I32), sorted_d.rearrange("(p k) c -> p (k c)", k=K)).then_inc(records_in, 16)
                sp.dma_start(prev_last[1:P, :],
                             sorted_d[0:(P - 1) * K, :].rearrange("(p k) c -> p (k c)", k=K)[:, (K - 1) * REC:(K - 1) * REC + 1],
                             allow_slow_non_contiguous=True).then_inc(records_in, 16)
                sp.wait_ge(edges_sorted, 1)
            store_runs(0, 0, HALF)
            store_group(0, HALF, 0)
            sp.wait_ge(bounds_ready, 1)
            sp.dma_start(end_d.rearrange("(h l) -> h l", l=LO), cum[:, :]).then_inc(bounds_out, 16)
            sp.dma_start(start_d.rearrange("(h l) -> h l", l=LO), hist_tmp[:, :]).then_inc(bounds_out, 16)
            sp.dma_start(end_idx_d.rearrange("(h l) -> h l", l=LO), hist_idx[:, :]).then_inc(bounds_out, 16)
            store_group(0, HALF, 1)
            sp.wait_ge(bounds_out, 48)
            sp.dma_start(end_idx[:, :], end_idx_d[0:NODES].rearrange("(a b) -> a b", b=NB)).then_inc(idx_in, 16)
            with sp.Fori(HALF + 1, TURNS - 1) as i:
                for s, (tile, d) in enumerate(((end_b, end_d), (start_b, start_d))):
                    store_group(0, i, s)
                    piece = bass.ds(i * PIECE - (HALF + 1) * PIECE, PIECE)
                    sp.dma_start(tile[:, piece],
                                 d[piece].rearrange("(o n) -> o n", o=1).broadcast_to([P, PIECE])).then_inc(bounds_in, 16)
            store_runs(0, TURNS - 1, TURNS)
            store_h(1)
            store_runs(1)
            store_xt(2)
            store_runs(2)
            store_xt(3)
            store_runs(3)
            o = out.rearrange("(a b) d -> a b d", b=NB)
            with sp.Fori(0, BLKS) as i:
                sp.wait_ge(res_ready, i + 1)
                for a, z in SPLIT:
                    sp.dma_start(o[a:z, bass.ds(i * BLK, BLK), :], res[a:z, :, :]).then_inc(res_out, 16)
            sp.wait_ge(res_out, 32 * BLKS + 1)
            for t in range(2):
                sp.wait_ge(table_out[t], 32 * BLKS + 1)
            sp.wait_ge(zero_out, 64)
            for s in range(SLOTS):
                sp.wait_ge(stored[s], 16 * N_STORES * TURNS * 4 + 1)
            for j in range(BLK):
                sp.wait_ge(xt_stored[j], 32 * BLKS * 2 + 1)

        @block.gpsimd
        def _(pool):
            made = Steps()

            def const(instruction):
                instruction.then_inc(consts_ready, 1)
                pool.wait_ge(consts_ready, made.next())

            const(pool.memset(dst_t[96:P, :], float(NODES)))
            const(pool.memset(src_t[96:P, :], 0.0))
            const(pool.memset(typ_t[96:P, :], 0.0))
            const(pool.memset(prev_last[:, :], -1.0))
            const(pool.memset(zero_row[:, :], 0.0))
            assert made.here == EDGE_CONSTS
            const(pool.memset(eps_c[:, :], LN_EPS))
            const(pool.memset(ones[:, :], 1.0))
            const(pool.affine_select(out=ident[:, :], in_=ones[:, :], compare_op=ALU.is_equal, fill=0.0, base=0,
                                     pattern=[[-1, P]], channel_multiplier=1))
            const(pool.affine_select(out=upper[:, :], in_=ones[0:HI, 0:HI], compare_op=ALU.is_gt, fill=0.0, base=0,
                                     pattern=[[1, HI]], channel_multiplier=-1))
            const(pool.iota(class_no[:, :, :], pattern=[[1, LO], [0, GROUP]], base=0, channel_multiplier=0,
                            allow_small_or_imprecise_dtypes=True))
            const(pool.iota(lo_edge[:, :], pattern=[[0, 1]], base=0, channel_multiplier=K,
                            allow_small_or_imprecise_dtypes=True))
            const(pool.iota(hi_edge[:, :], pattern=[[0, 1]], base=K, channel_multiplier=K,
                            allow_small_or_imprecise_dtypes=True))
            const(pool.affine_select(out=before_w[:, :], in_=ones[:, :], compare_op=ALU.is_gt, fill=0.0, base=0,
                                     pattern=[[1, P]], channel_multiplier=-1))
            const(pool.affine_select(out=after_w[:, :], in_=ones[:, :], compare_op=ALU.is_ge, fill=0.0, base=0,
                                     pattern=[[-1, P]], channel_multiplier=1))
            const(pool.iota(tile_no[:, :, :], pattern=[[1, NB], [0, P]], base=0, channel_multiplier=0,
                            allow_small_or_imprecise_dtypes=True))
            const(pool.iota(lane_base[:, :], pattern=[[0, 1]], base=0, channel_multiplier=-NB,
                            allow_small_or_imprecise_dtypes=True))
            assert made.here == CONSTS

            def gather_runs(l):
                with pool.Fori(0, TURNS) as i:
                    for s in range(SLOTS):
                        g = i * SLOTS + s
                        pool.wait_ge(idx_staged, g + (SLOTS * TURNS * l + 1))
                        pool.wait_ge(stored[s], i * (16 * N_STORES) + (16 * N_STORES * TURNS * l + 1))
                        pool.wait_ge(scan_done, g * GROUP + (CREDIT + K * l - GROUP + 4))
                        pool.sem_inc(group_begun, 1)
                        for q, (k0, kn) in enumerate(LANDS[KIND[l]]):
                            for k in range(k0, k0 + kn):
                                pool.indirect_dma_start(
                                    out=ring[:, s, k, :], out_offset=None, in_=table[l],
                                    in_offset=bass.IndirectOffsetOnAxis(ap=idx_ring[:, s, k:k + 1], axis=0),
                                ).then_inc(landed[KIND[l]][s][q], 16)

            def gather_ends(l):
                for s in range(SLOTS):
                    pool.wait_ge(stored[s], 16 * N_STORES * TURNS * (l + 1) + 1)
                if l == 0:
                    pool.wait_ge(zero_out, 64)
                    pool.wait_ge(idx_in, 16)
                else:
                    pool.wait_ge(agg_ready, BLKS * l + 1)
                for b in range(NB):
                    i, j = b // BLK, b % BLK
                    if i:
                        pool.wait_ge(end_row[j], 16 * (BLKS * l + i))
                    pool.indirect_dma_start(
                        out=ends[:, b, :], out_offset=None, in_=run_rows[l],
                        in_offset=bass.IndirectOffsetOnAxis(ap=end_idx[:, b:b + 1], axis=0),
                    ).then_inc(end_row[j], 16)

            with pool.If(unsorted(pool) != 0):
                pool.wait_ge(part2, 1)
                pool.iota(end_w[:, 0:CLASSES], pattern=[[1, CLASSES]], base=0, channel_multiplier=0,
                          allow_small_or_imprecise_dtypes=True).then_inc(classes_ready, 1)
                with pool.Fori(0, K) as i:
                    pool.wait_ge(record_ready, i + 1)
                    pool.sem_inc(group_begun, 1)
                    pool.indirect_dma_start(
                        out=sorted_d, out_offset=bass.IndirectOffsetOnAxis(ap=pos[:, :], axis=0),
                        in_=record[:, :], in_offset=None).then_inc(record_out, 16)
                    pool.wait_ge(record_out, i * 16 + 16)
                    pool.sem_inc(record_free, 1)
                pool.wait_ge(edges_sorted, 1)
            for l in range(4):
                if l < 2:
                    pool.wait_ge(table_out[l], 32 * BLKS + 1)
                else:
                    for j in range(BLK):
                        pool.wait_ge(xt_stored[j], 32 * BLKS * (l - 1) + 1)
                gather_runs(l)
                gather_ends(l)

        @block.scalar
        def _(act):
            def stage_idx(l):
                with act.Fori(0, TURNS) as i:
                    for s in range(SLOTS):
                        g = i * SLOTS + s
                        act.wait_ge(scan_done, g * GROUP + (K * l + CREDIT - GROUP))
                        act.copy(idx_ring[:, s, :], run_idx(l)[:, bass.ds(g * GROUP, GROUP)]).then_inc(idx_staged, 1)

            def split_h(t):
                act.wait_ge(h_kept, BLKS * (t + 1) + 1)
                act.copy(h_parts[:, :, 0, :], h_all).then_inc(part0, 1)
                act.wait_ge(rest_ready, t + 1)
                act.copy(h_parts[:, :, 1, :], h_all).then_inc(part1, 1)

            def stage_src(l, g, s):
                act.wait_ge(scan_done, g * GROUP + (K * l + CREDIT - GROUP))
                act.copy(idx_ring[:, s, :], src_t[:, bass.ds(g * GROUP, GROUP)]).then_inc(idx_staged, 1)
                act.copy(src_cols[:, s, :],
                         src_t[:, bass.ds(g * GROUP + PE_FIRST, PE_STEPS)]).then_inc(src_staged, 1)

            def offsets(l, g):
                act.wait_ge(src_spread, g + (GROUPS * l + 1))
                act.wait_ge(src_hot_made, g * PE_STEPS + (GROUPS * PE_STEPS * l + 1))
                act.activation(src_off[:, :, :], ps_src, ACT.Identity, bias=lane_base[:, :]).then_inc(off_ready, 1)

            def stage_groups(l):
                with act.Fori(0, TURNS - 1) as i:
                    for s in range(SLOTS):
                        offsets(l, i * SLOTS + s)
                        stage_src(l, i * SLOTS + s + 1, 1 - s)
                offsets(l, GROUPS - 2)
                stage_src(l, GROUPS - 1, 1)
                offsets(l, GROUPS - 1)

            def blocks(t):
                per, base = {0: (1, 0), 1: (1, BLKS), 2: (2, 2 * BLKS)}.get(t, (0, 0))

                def copy_products(before, tiles):
                    for j in tiles:
                        m = before * BLK + (NB * (t - 2) + j)
                        act.wait_ge(xt_stored[j], before * 32 + (32 * BLKS * (t - 2) + 1))
                        for half, (full, copied) in enumerate(((xta_full, xta_sb), (xtb_full, xtb_sb))):
                            act.wait_ge(full, m + 1)
                            act.copy(xt_out[:, j, half * 512:half * 512 + 512],
                                     ps[0:NA, 6 + half, :]).then_inc(copied, 1)

                def root(k, r, layer_norm):
                    act.wait_ge(sq_ready, k * per + (base + r + 1))
                    if layer_norm:
                        act.activation(st[:, 2, :], st[:, 1, :], ACT.Sqrt, bias=eps_c[:, :],
                                       scale=1.0 / D).then_inc(root_ready, 1)
                    else:
                        act.activation(st[:, 2, :], st[:, 1, :], ACT.Sqrt).then_inc(root_ready, 1)

                def turn(before, k, ahead):
                    products = t >= 2 and before is not None
                    if k is not None and t in (0, 1, 2):
                        root(k, 0, t == 0)
                    if products:
                        copy_products(before, (0,))
                    if ahead is not None and t in (1, 2):
                        act.wait_ge(agg_t_full, ahead + (BLKS * (t - 1) + 1))
                        act.copy(agg_t[:, :, 0:NA], ps_t[:, :, 0:NA]).then_inc(agg_t_sb, 1)
                    if products:
                        copy_products(before, (1, 2))
                    if k is not None and t == 2:
                        root(k, 1, True)
                    if products:
                        copy_products(before, (3, 4))
                    if k is not None:
                        act.wait_ge(h_t_full, k + (BLKS * t + 2))
                        act.copy(h_tr[:, :, 0:NA], ps_t[:, :, 0:NA]).then_inc(h_t_sb, 1)
                        if t < 2:
                            act.copy(h_all[:, bass.ds(k * BLK, BLK), :], h_t[:, :, :]).then_inc(h_kept, 1)

                pipeline(act, turn)

            act.wait_ge(consts_ready, CONSTS)
            blocks(0)
            act.wait_ge(edges_in, 16 * 10)
            violations = unsorted(act)
            with act.If(violations != 0):
                split_h(0)
                act.wait_ge(edges_sorted, 1)
            stage_src(0, 0, 0)
            with act.If(violations == 0):
                split_h(0)
            stage_groups(0)
            blocks(1)
            stage_src(1, 0, 0)
            split_h(1)
            stage_groups(1)
            blocks(2)
            act.wait_ge(idx_ready, 1)
            stage_idx(2)
            blocks(3)
            stage_idx(3)

        @block.tensor
        def _(pe):
            def count_before():
                chunks = [(c, min(512, CLASSES - c)) for c in range(0, CLASSES, 512)]

                def add(weights, start):
                    for c, width in chunks:
                        mm = pe.matmul(ps_seen[:, c:c + width], weights[:, :], hot[:, c:c + width],
                                       start=start, stop=True, skip_group_check=True)
                    return mm

                pe.wait_ge(sort_begun, 1)
                add(before_w, True).then_inc(seen_cleared, 1)
                with pe.Fori(0, K) as i:
                    pe.wait_ge(hot_made, i + 1)
                    add(before_w, False).then_inc(ranked, 1)
                    pe.wait_ge(rank_read, i + 1)
                    add(after_w, False).then_inc(counted, 1)

            def count_group(c):
                pe.wait_ge(hot_ready, c * 2 + 2)
                pe.wait_ge(hist_added, c + 1)
                for k in range(GROUP):
                    mm = pe.matmul(ps_hist, hot_hi[:, :, k], hot_lo[:, :, k],
                                   start=(k == 0), stop=(k == GROUP - 1))
                mm.then_inc(hist_part, 1)

            def spread_sources(l, g, s):
                pe.wait_ge(src_staged, g + (GROUPS * l + 1))
                pe.wait_ge(off_ready, g + (GROUPS * l + 1))
                for m in range(PE_STEPS):
                    mm = pe.matmul(ps_src[:, m, :], src_cols[:, s, m:m + 1].broadcast_to([P, NA]), ident[:, :],
                                   start=True, stop=True)
                mm.then_inc(src_spread, 1)

            def fetch_group(l, i, s, more, counts=False):
                g = i * SLOTS + s
                for m in range(PE_STEPS):
                    if m == PE_STEPS - 1 and more:
                        spread_sources(l, g + 1, 1 - s)
                    n = g * PE_STEPS + (GROUPS * PE_STEPS * l + m)
                    pe.wait_ge(src_hot_made, n + 2)
                    pe.wait_ge(scan_done, g * GROUP + (K * l + CREDIT - GROUP))
                    for b in range(NB):
                        for part in range(3):
                            mm = pe.matmul(ps_rows[s][:, m, :], src_hot[:, (PE_STEPS * s + m) % 2, b, :], h_parts[:, b, part, :],
                                           start=(b == 0 and part == 0), stop=(b == NB - 1 and part == 2))
                    mm.then_inc(rows_fetched, 1)
                    if counts and m == 2:
                        count_group(g * 2)
                    if counts and m == 4:
                        count_group(g * 2 + 1)

            def fetch(l):
                pe.wait_ge(part2, l + 1)
                pe.wait_ge(self_sb, BLKS * (l + 1) + 1)
                pe.wait_ge(h_t_sb, BLKS * (l + 1))
                spread_sources(l, 0, 0)
                if l == 0:
                    with pe.Fori(0, HALF) as i:
                        for s in range(SLOTS):
                            fetch_group(l, i, s, True, counts=True)
                    fetch_group(l, HALF, 0, True, counts=True)
                    pe.wait_ge(tot_ready, 1)
                    pe.matmul(ps_small[0:HI, 0:1], upper[:, :], cum[:, LO - 1:LO],
                              start=True, stop=True).then_inc(base_ready, 1)
                    fetch_group(l, HALF, 1, True)
                with pe.Fori(HALF + 1 if l == 0 else 0, TURNS - 1) as i:
                    for s in range(SLOTS):
                        fetch_group(l, i, s, True)
                for s in range(SLOTS):
                    fetch_group(l, TURNS - 1, s, s < SLOTS - 1)

            def carries(l):
                pe.wait_ge(last_copied, l + 1)
                pe.transpose(ps_t[:, 0, :], last_rows[:, :], ident[:, :]).then_inc(last_t, 1)
                pe.wait_ge(carry_scanned, l + 1)
                pe.transpose(ps_t[:, 1, :], carry_t[:, :], ident[:, :]).then_inc(carry_back, 1)
                pe.wait_ge(carry_split, l + 1)

            def blocks(t):
                def self_product(before, k):
                    if k is not None and t in (1, 2):
                        pe.wait_ge(prod_read, k + (BLKS * (t - 1) + 1))
                    pe.wait_ge(h_t_sb, before + (BLKS * t + 1))
                    pe.wait_ge(self_sb, before + (BLKS * t + 1))
                    for j in range(BLK):
                        mm = pe.matmul(ps_o[0:NA, j, :], h_tr[:, j, 0:NA], w_self[t][:, :],
                                       start=True, stop=True)
                    mm.then_inc(self_full, 1)

                def products(before, tiles):
                    for j in tiles:
                        m = before * BLK + (NB * (t - 2) + j)
                        for half, (full, copied) in enumerate(((xta_full, xta_sb), (xtb_full, xtb_sb))):
                            pe.wait_ge(copied, m + 1)
                            pe.matmul(ps[0:NA, 6 + half, :], h_tr[:, j, 0:NA],
                                      w_rel[t][:, 4 * half:4 * half + 4, :].rearrange("d r e -> d (r e)"),
                                      start=True, stop=True).then_inc(full, 1)

                def turn(before, k, ahead):
                    pending = t in (2, 3) and before is not None
                    if ahead is not None and t >= 1:
                        n = ahead + (BLKS * (t - 1) + 1)
                        pe.wait_ge(agg_ready, n)
                        for j in range(BLK):
                            for part in range(3):
                                mm = pe.matmul(ps_c[0:NA, j, :],
                                               span[:, bass.ds(ahead * BLK + j, 1), :].rearrange("p o a -> p (o a)"),
                                               carry_parts[:, part, :], start=(part == 0), stop=(part == 2))
                        mm.then_inc(c_full, 1)
                    if before is not None and t < 4:
                        self_product(before, k)
                    if pending:
                        products(before, (0,))
                    if ahead is not None and t in (1, 2):
                        pe.wait_ge(agg_ready, n + 1)
                        for j in range(BLK):
                            mm = pe.transpose(ps_t[:, j, 0:NA], agg[:, j, :], ident[0:NA, 0:NA])
                        mm.then_inc(agg_t_full, 1)
                    if pending:
                        products(before, (1,))
                    if ahead is not None and t in (1, 2):
                        pe.wait_ge(agg_t_sb, n)
                        pe.wait_ge(self_sb, BLKS * t + 1 if before is None else before + (BLKS * t + 2))
                        if k is not None:
                            pe.wait_ge(prod_read, k + (BLKS * (t - 1) + 1))
                        for j in range(BLK):
                            mm = pe.matmul(ps_o[0:NA, j, :], agg_t[:, j, 0:NA], w_l[t][:, :], start=True, stop=True)
                        mm.then_inc(prod_full, 1)
                    if pending:
                        products(before, (2, 3, 4))
                    if k is not None and t < 4:
                        pe.wait_ge(h_ready, k + (BLKS * t + 1))
                        for j in range(BLK):
                            mm = pe.transpose(ps_t[:, j, 0:NA], h_t[:, j, :], ident[0:NA, 0:NA])
                        mm.then_inc(h_t_full, 1)

                pipeline(pe, turn)

            pe.wait_ge(consts_ready, CONSTS)
            pe.wait_ge(weights_in, 16 * N_WEIGHTS)
            blocks(0)
            pe.wait_ge(unsorted_ready, 1)
            pe.matmul(ps_small[0:1, 0:1], ones[:, 0:1], unsorted_p[:, 0:1], start=True, stop=True).then_inc(check_sum, 1)
            with pe.If(unsorted(pe) != 0):
                count_before()
                pe.wait_ge(edges_sorted, 1)
            pe.wait_ge(passes_ready, 1)
            pe.matmul(ps_passes, passes_w[:, :], ident[:, :], start=True, stop=True).then_inc(passes_bc, 1)
            fetch(0)
            for t in range(1, 5):
                carries(t - 1)
                if t == 1:
                    pe.wait_ge(span_ready, 1)
                blocks(t)
                if t == 1:
                    fetch(1)

        @block.vector
        def _(dve):
            v = Steps()

            def step(instruction):
                instruction.then_inc(vec, 1)
                dve.wait_ge(vec, v.next())

            def over(column):
                return column.unsqueeze(2).broadcast_to([NA, BLK, D])

            def blocks(t):
                op = ALU.max if t < 3 else ALU.add

                def add_carries(ahead):
                    for j in range(BLK):
                        dve.wait_ge(end_row[j], ahead * 16 + 16 * (BLKS * (t - 1) + 1))
                    dve.wait_ge(c_full, ahead + (BLKS * (t - 1) + 1))
                    dve.tensor_tensor(agg[:, :, :], ends[:, bass.ds(ahead * BLK, BLK), :], ps_c[0:NA, :, :],
                                      op).then_inc(agg_ready, 1)

                def add_self(before):
                    dve.wait_ge(weights_in, 16 * N_WEIGHTS)
                    dve.wait_ge(self_full, before + (BLKS * t + 1))
                    dve.tensor_tensor(self_all[:, bass.ds(before * BLK, BLK), :], ps_o[0:NA, :, :],
                                      b_self[t][:, :].unsqueeze(1).broadcast_to([NA, BLK, D]),
                                      ALU.add).then_inc(self_sb, 1)
                    dve.wait_ge(self_sb, before + (BLKS * t + 2))

                def turn(before, k, ahead):
                    roots = {0: (1, 0), 1: (1, BLKS), 2: (2, 2 * BLKS)}.get(t)

                    def others():
                        if ahead is not None and t >= 1:
                            add_carries(ahead)
                        if before is not None and t < 4:
                            add_self(before)

                    if k is None:
                        others()
                        return
                    tiles = bass.ds(k * BLK, BLK)
                    xs, selfs = x_all[:, tiles, :], self_all[:, tiles, :]
                    n = k + (BLKS * (t - 1) + 1)
                    if t in (1, 2):
                        dve.wait_ge(prod_full, n)
                        dve.wait_ge(h_ready, k + BLKS * t)
                        dve.tensor_tensor(o_t[:, :, :], ps_o[0:NA, :, :], selfs, ALU.add).then_inc(prod_read, 1)
                        dve.wait_ge(prod_read, n)
                        step(dve.tensor_tensor(sq_t[:, :, :], o_t[:, :, :], o_t[:, :, :], ALU.mult))
                        dve.tensor_reduce(st[:, 1, :], sq_t[:, :, :], AX.X, ALU.add).then_inc(sq_ready, 1)
                        others()
                        dve.wait_ge(root_ready, k * roots[0] + (roots[1] + 1))
                        step(dve.tensor_scalar(st[:, 3, :], st[:, 2, :], NORM_EPS, None, ALU.max))
                        step(dve.reciprocal(st[:, 3, :], st[:, 3, :]))
                    if t == 2:
                        step(dve.scalar_tensor_tensor(out=o_t[:, :, :], in0=o_t[:, :, :], scalar=0.0,
                                                      in1=over(st[:, 3, :]), op0=ALU.max, op1=ALU.mult))
                        step(dve.tensor_tensor(xs, xs, o_t[:, :, :], ALU.add))
                        dve.sem_inc(x_added, 1)
                    if t in (0, 2):
                        if t == 0:
                            dve.wait_ge(x_first_in if before is None else x_in, 32)
                        step(dve.tensor_reduce(st[:, 0, :], xs, AX.X, ALU.add))
                        step(dve.tensor_scalar(st[:, 0, :], st[:, 0, :], -1.0 / D, None, ALU.mult))
                        step(dve.tensor_tensor(cen[:, :, :], xs, over(st[:, 0, :]), ALU.add))
                        step(dve.tensor_tensor(sq_t[:, :, :], cen[:, :, :], cen[:, :, :], ALU.mult))
                        dve.tensor_reduce(st[:, 1, :], sq_t[:, :, :], AX.X, ALU.add).then_inc(sq_ready, 1)
                        if t == 0:
                            others()
                        dve.wait_ge(root_ready, k * roots[0] + (roots[1] + roots[0]))
                        step(dve.reciprocal(st[:, 3, :], st[:, 2, :]))
                    if t in (3, 4):
                        dve.wait_ge(agg_ready, n + 1)
                        step(dve.tensor_tensor(o_t[:, :, :], agg[:, :, :], selfs, ALU.add))
                    if t < 4:
                        dve.wait_ge(h_t_full, k + (BLKS * t + 1))
                        if t < 2:
                            dve.wait_ge(table_out[t], k * 32 + 1)
                            dve.wait_ge(h_kept, k + (BLKS * t + 1))
                        if t == 3:
                            dve.tensor_scalar(h_t[:, :, :], o_t[:, :, :], 0.0, None, ALU.max).then_inc(h_ready, 1)
                        else:
                            raw = o_t if t == 1 else cen
                            dve.scalar_tensor_tensor(out=h_t[:, :, :], in0=raw[:, :, :], scalar=0.0,
                                                     in1=over(st[:, 3, :]), op0=ALU.max,
                                                     op1=ALU.mult).then_inc(h_ready, 1)
                    if t == 4:
                        dve.wait_ge(res_out, k * 32 + 1)
                        dve.scalar_tensor_tensor(out=res[:, :, :], in0=o_t[:, :, :], scalar=0.0, in1=xs,
                                                 op0=ALU.max, op1=ALU.add).then_inc(res_ready, 1)
                    if t in (3, 4):
                        others()

                pipeline(dve, turn, v, {0: 5, 1: 3, 2: 10, 3: 1, 4: 1}[t])

            def split_h(t):
                dve.wait_ge(part0, t + 1)
                dve.tensor_tensor(h_all, h_all, h_parts[:, :, 0, :], ALU.subtract).then_inc(rest_ready, 1)
                dve.wait_ge(part1, t + 1)
                dve.tensor_tensor(h_parts[:, :, 2, :], h_all, h_parts[:, :, 1, :], ALU.subtract).then_inc(part2, 1)

            def one_hots(g):
                dve.wait_ge(hist_part, g + 1)
                for hot, part, n in ((hot_hi, dst_hi, HI), (hot_lo, dst_lo, LO)):
                    dve.tensor_tensor(hot[:, :, :],
                                      part[:, bass.ds(g * GROUP, GROUP)].unsqueeze(1).broadcast_to([P, n, GROUP]),
                                      class_no[:, 0:n, :], ALU.is_equal).then_inc(hot_ready, 1)

            def scan_steps(l, g, s, k0, kn):
                for k in range(k0, k0 + kn):
                    before = ring[:, s, k - 1, :] if k else ring[:, 1 - s, GROUP - 1, :]
                    row = ps_rows[s][:, k - PE_FIRST, :] if l < 2 and k >= PE_FIRST else ring[:, s, k, :]
                    if l < 2 and k >= PE_FIRST:
                        m = min(BANK_STEPS, PE_STEPS) if k - PE_FIRST < BANK_STEPS else PE_STEPS
                        dve.wait_ge(rows_fetched, g * PE_STEPS + (GROUPS * PE_STEPS * l + m + 2))
                    at = g * GROUP + k
                    dve.wait_ge(scan_done, at + (CREDIT + K * l))
                    dve.scalar_tensor_tensor(out=ring[:, s, k, :], in0=before, scalar=same[:, bass.ds(at, 1)],
                                             in1=row, op0=ALU.mult,
                                             op1=ALU.max if l < 2 else ALU.add).then_inc(scan_done, 1)

            def scan_landed(l, i, s, q):
                kind = KIND[l]
                k0, kn = LANDS[kind][q]
                dve.wait_ge(landed[kind][s][q], i * (16 * kn) + 16 * kn * (TURNS * (l % 2) + 1))
                scan_steps(l, i * SLOTS + s, s, k0, kn)

            def hot_sources(l, g, s, m):
                n = g * PE_STEPS + (GROUPS * PE_STEPS * l + m)
                dve.wait_ge(off_ready, g + (GROUPS * l + 2))
                dve.wait_ge(rows_fetched, n + 1)
                dve.tensor_tensor(src_hot[:, (PE_STEPS * s + m) % 2, :, :],
                                  src_off[:, m, :].unsqueeze(1).broadcast_to([NA, NB, P]), tile_no[:, :, :],
                                  ALU.is_equal).then_inc(src_hot_made, 1)

            def add_histogram(c):
                dve.wait_ge(hist_part, c + 2)
                dve.tensor_tensor(hist[:, :], hist[:, :], ps_hist, ALU.add).then_inc(hist_added, 1)
                dve.wait_ge(hist_added, c + 2)

            def scan_max_group(l, i, s, more, counts=False):
                g = i * SLOTS + s
                for q in range(len(LANDS["max"])):
                    scan_landed(l, i, s, q)
                    m = q + 2
                    if m < PE_STEPS:
                        hot_sources(l, g, s, m)
                    elif more:
                        hot_sources(l, g + 1, 1 - s, m - PE_STEPS)
                    if counts and q == 0:
                        one_hots(g * 2)
                    if counts and q == 2:
                        add_histogram(g * 2)
                        one_hots(g * 2 + 1)
                if counts:
                    add_histogram(g * 2 + 1)
                scan_steps(l, g, s, PE_FIRST, PE_STEPS)

            def scan_max(l):
                if l:
                    dve.wait_ge(agg_ready, BLKS * l + 1)
                hot_sources(l, 0, 0, 0)
                hot_sources(l, 0, 0, 1)
                if l == 0:
                    with dve.Fori(0, HALF) as i:
                        for s in range(SLOTS):
                            scan_max_group(l, i, s, True, counts=True)
                    scan_max_group(l, HALF, 0, True, counts=True)
                    node_bounds()
                    scan_max_group(l, HALF, 1, True)
                with dve.Fori(HALF + 1 if l == 0 else 0, TURNS - 1) as i:
                    for s in range(SLOTS):
                        scan_max_group(l, i, s, True)
                if l == 0:
                    spans()
                for s in range(SLOTS):
                    scan_max_group(l, TURNS - 1, s, s < SLOTS - 1)

            def scan_sum(l):
                with dve.Fori(0, TURNS) as i:
                    for s in range(SLOTS):
                        for q in range(len(LANDS["sum"])):
                            scan_landed(l, i, s, q)

            def keep_last(l):
                dve.wait_ge(scan_done, CREDIT + K * (l + 1))
                dve.tensor_copy(last_rows[:, :], ring[:, SLOTS - 1, GROUP - 1, :]).then_inc(last_copied, 1)

            def node_bounds():
                step(dve.tensor_tensor_scan(cum[:, :], ones[0:HI, 0:LO], hist[:, :], 0.0, ALU.mult, ALU.add))
                dve.sem_inc(tot_ready, 1)
                dve.wait_ge(base_ready, 1)
                step(dve.tensor_copy(hist_base[:, :], ps_small[0:HI, 0:1]))
                step(dve.tensor_scalar(cum[:, :], cum[:, :], hist_base[:, :], -1.0, ALU.add, ALU.add))
                step(dve.scalar_tensor_tensor(out=hist_tmp[:, :], in0=cum[:, :], scalar=1.0, in1=hist[:, :],
                                              op0=ALU.add, op1=ALU.subtract))
                step(dve.tensor_scalar(hist_new[:, :], cum[:, :], -1.0, float(EMPTY_ROW), ALU.mult, ALU.add))
                step(dve.scalar_tensor_tensor(out=hist_new[:, :], in0=hist[:, :], scalar=0.0, in1=hist_new[:, :],
                                              op0=ALU.is_equal, op1=ALU.mult))
                dve.tensor_tensor(hist_idx[:, :], hist_new[:, :], cum[:, :], ALU.add).then_inc(bounds_ready, 1)

            def spans():
                dve.wait_ge(bounds_in, 32 * (TURNS - 2 - HALF))
                step(dve.tensor_scalar(hit, end_b, hi_edge[:, :], None, ALU.is_lt))
                step(dve.scalar_tensor_tensor(out=hit, in0=end_b, scalar=lo_edge[:, :], in1=hit,
                                              op0=ALU.is_ge, op1=ALU.mult))
                dve.scalar_tensor_tensor(out=span[:, :, :].rearrange("p b a -> p a b"),
                                         in0=start_b.rearrange("p (a b) -> p a b", b=NB),
                                         scalar=lo_edge[:, :],
                                         in1=hit.rearrange("p (a b) -> p a b", b=NB),
                                         op0=ALU.is_lt, op1=ALU.mult).then_inc(span_ready, 1)

            def carries(l):
                dve.wait_ge(last_t, l + 1)
                dve.tensor_tensor_scan(carry_t[:, 1:P], passes_b[:, 0:P - 1], ps_t[:, 0, 0:P - 1], 0.0,
                                       ALU.mult, ALU.max if l < 2 else ALU.add).then_inc(carry_scanned, 1)
                dve.wait_ge(carry_back, l + 1)
                step(dve.tensor_copy(carry_parts[:, 0, :], ps_t[:, 1, :]))
                step(dve.tensor_tensor(carry[:, :], ps_t[:, 1, :], carry_parts[:, 0, :], ALU.subtract))
                step(dve.tensor_copy(carry_parts[:, 1, :], carry[:, :]))
                step(dve.tensor_tensor(carry_r[:, :], carry[:, :], carry_parts[:, 1, :], ALU.subtract))
                dve.tensor_copy(carry_parts[:, 2, :], carry_r[:, :]).then_inc(carry_split, 1)

            def sort_edges():
                w = Steps()

                def sort_step(instruction):
                    instruction.then_inc(sort_vec, 1)
                    dve.wait_ge(sort_vec, w.next())

                dve.memset(hot[:, :], 0.0).then_inc(sort_begun, 1)
                sort_step(dve.tensor_copy(dst_f[:, :], dst_t[:, :]))
                dve.wait_ge(seen_cleared, 1)
                dve.wait_ge(classes_ready, 1)
                with dve.Fori(0, K) as i:
                    w.loop(i, 3)
                    dve.wait_ge(counted, i + 1)
                    dve.tensor_scalar(hot[:, :], end_w[:, 0:CLASSES], dst_f[:, bass.ds(i, 1)], None,
                                      ALU.is_equal).then_inc(hot_made, 1)
                    dve.wait_ge(hot_made, i + 1)
                    dve.wait_ge(ranked, i + 1)
                    sort_step(dve.tensor_tensor(hit_w[:, 0:CLASSES], ps_seen, hot[:, :], ALU.mult))
                    sort_step(dve.tensor_reduce(col[:, :], hit_w[:, 0:CLASSES], AX.X, ALU.add))
                    sort_step(dve.tensor_scalar(rank[:, bass.ds(i, 1)], col[:, :], 0.0, None, ALU.add))
                    dve.sem_inc(rank_read, 1)
                w.end_loop(K)
                dve.wait_ge(counted, K + 1)
                sort_step(dve.memset(hit_w[:, 0:CLASSES], 1.0))
                sort_step(dve.tensor_tensor_scan(start_w[:, :], hit_w[:, 0:CLASSES], ps_seen, 0.0, ALU.mult, ALU.add))
                sort_step(dve.tensor_tensor(start_w[:, :], start_w[:, :], ps_seen, ALU.subtract))
                with dve.Fori(0, K) as i:
                    w.loop(i, 6)
                    sort_step(dve.scalar_tensor_tensor(out=hit_w[:, 0:CLASSES], in0=end_w[:, 0:CLASSES],
                                                  scalar=dst_f[:, bass.ds(i, 1)], in1=start_w[:, :],
                                                  op0=ALU.is_equal, op1=ALU.mult))
                    sort_step(dve.tensor_reduce(col[:, :], hit_w[:, 0:CLASSES], AX.X, ALU.add))
                    dve.wait_ge(record_free, i + 1)
                    sort_step(dve.tensor_scalar(pos[:, :], rank[:, bass.ds(i, 1)], col[:, :], None, ALU.add))
                    for c, tile in enumerate((dst_t, src_t, typ_t)):
                        sort_step(dve.tensor_scalar(record[:, c:c + 1], tile[:, bass.ds(i, 1)], 0.0, None, ALU.add))
                    dve.sem_inc(record_ready, 1)
                w.end_loop(K)
                dve.wait_ge(records_in, 32)
                for c, tile in enumerate((dst_t, src_t, typ_t)):
                    sort_step(dve.tensor_copy(tile[:, :], hit_w[:, :].bitcast(I32).rearrange("p (k c) -> p k c", c=REC)[:, :, c]))
                dve.sem_inc(edges_sorted, 1)

            for free in (agg_ready, xta_sb, xtb_sb, h_t_full, table_out[0], table_out[1], res_out, hist_part,
                         hist_added, counted, record_free, self_sb, h_kept, *stored, *xt_stored):
                dve.sem_inc(free, 1)
            dve.sem_inc(scan_done, CREDIT)
            dve.sem_inc(off_ready, 1)
            dve.sem_inc(src_hot_made, 1)
            dve.sem_inc(rows_fetched, 2)
            step(dve.memset(ring[:, SLOTS - 1, GROUP - 1, :], 0.0))
            step(dve.memset(hist[:, :], 0.0))
            step(dve.memset(carry_t[:, 0:1], 0.0))
            step(dve.memset(record[:, :], 0))

            blocks(0)

            dve.wait_ge(consts_ready, CONSTS)
            dve.wait_ge(edges_in, 16 * 10)
            step(dve.tensor_tensor(hit_w[:, 0:K - 1], dst_t[:, 1:K], dst_t[:, 0:K - 1], ALU.is_lt))
            step(dve.tensor_reduce(unsorted_p[:, 0:1], hit_w[:, 0:K - 1], AX.X, ALU.add))
            step(dve.tensor_tensor(unsorted_p[:, 1:2], dst_t[:, 0:1], prev_last[:, :], ALU.is_lt))
            dve.tensor_tensor(unsorted_p[:, 0:1], unsorted_p[:, 0:1], unsorted_p[:, 1:2], ALU.add).then_inc(unsorted_ready, 1)
            dve.wait_ge(check_sum, 1)
            dve.tensor_copy(unsorted_i[:, :], ps_small[0:1, 0:1]).then_inc(check_int, 1)

            split_h(0)
            with dve.If(unsorted(dve) != 0):
                sort_edges()
            dve.scalar_tensor_tensor(out=rel_idx[:, :], in0=src_t[:, :], scalar=float(RELS), in1=typ_t[:, :],
                                     op0=ALU.mult, op1=ALU.add).then_inc(idx_ready, 1)
            dve.wait_ge(idx_ready, 1)
            step(dve.memset(same[:, 0:1], 0.0))
            step(dve.tensor_tensor(same[:, 1:K], dst_t[:, 1:K], dst_t[:, 0:K - 1], ALU.is_equal))
            for part, operand, op in ((dst_hi, LO.bit_length() - 1, ALU.logical_shift_right), (dst_lo, LO - 1, ALU.bitwise_and)):
                step(dve.tensor_scalar(dst_part, dst_t[:, :], operand, None, op))
                step(dve.tensor_copy(part[:, :], dst_part))
            step(dve.tensor_tensor(passes[:, :], dst_t[:, 0:1], prev_last[:, :], ALU.is_equal))
            step(dve.tensor_copy(passes_last[:, :], dst_t[:, K - 1:K]))
            step(dve.scalar_tensor_tensor(out=passes[:, :], in0=dst_t[:, 0:1], scalar=passes_last[:, :],
                                          in1=passes[:, :], op0=ALU.is_equal, op1=ALU.mult))
            dve.tensor_scalar(passes_w[:, :], ones[:, :], passes[:, :], None, ALU.mult).then_inc(passes_ready, 1)
            dve.wait_ge(passes_bc, 1)
            step(dve.tensor_copy(passes_b[:, :], ps_passes))
            for l in range(4):
                if l < 2:
                    scan_max(l)
                else:
                    scan_sum(l)
                keep_last(l)
                carries(l)
                blocks(l + 1)
                if l == 0:
                    split_h(1)


INPUTS = ["x", "src", "dst", "edge_type_8", "L0_gnn_W_l1", "L0_gnn_W_r1", "L0_gnn_b1", "L0_gnn_W_l2", "L0_gnn_W_r2",
          "L0_gnn_b2", "L1_gnn_w1", "L1_gnn_sl1", "L1_gnn_b1", "L1_gnn_w2", "L1_gnn_sl2", "L1_gnn_b2"]


def kernel(**inputs):
    import numpy as np
    import concourse.bacc as bacc
    from concourse.bass_utils import run_bass_kernel_spmd

    nc = bacc.Bacc("TRN2", target_bir_lowering=False, num_devices=1)
    arrays, args = {}, []
    for name in INPUTS:
        a = np.ascontiguousarray(inputs[name])
        arrays[f"in_{name}"] = a
        args.append(nc.dram_tensor(f"in_{name}", a.shape, mybir.dt.from_np(a.dtype), kind="ExternalInput").ap())
    out = nc.dram_tensor("out", (NODES, D), F32, kind="ExternalOutput").ap()
    build(nc, *args, out)
    return run_bass_kernel_spmd(nc, [arrays], core_ids=[0]).results[0]["out"]
```

```python
from contextlib import ExitStack

import concourse.bass as bass
from concourse import mybir

F32 = mybir.dt.float32
BF16 = mybir.dt.bfloat16
I32 = mybir.dt.int32
ALU = mybir.AluOpType
ACT = mybir.ActivationFunctionType
AX = mybir.AxisListType

P = 128
D = 128
NODES = 3125
NA, NB = 125, 25
EDGES = 103125
K = -(-EDGES // P)
TAIL = EDGES - (P - 1) * K
RELS = 8
GROUP = 31
SLOTS = 2
TURNS = K // (GROUP * SLOTS)
PE_STEPS = {"max": 5, "sum": 4}
BANK_STEPS = 4
MAX_STEPS, SUM_STEPS = PE_STEPS["max"], PE_STEPS["sum"]
LANDS = {"max": [(0, 5), (5, 5), (10, 5), (15, 6), (21, 5)],
         "sum": [(0, 7), (7, 7), (14, 8), (22, 5)]}
STORES = {"max": [(0, 8), (8, 9), (17, 9), (26, 5)], "sum": [(0, 8), (8, 8), (16, 8), (24, 7)]}
KIND = ["max", "max", "sum", "sum"]
GROUPS = K // GROUP
HALF = TURNS // 2
BLK = 5
BLKS = NB // BLK
HOT_PIECES = 5
HI, LO = 49, 64
SPANS_TURN = TURNS - 2
PIECES = SPANS_TURN - HALF - 1
PIECE = HI * LO // PIECES
CLASSES = NODES + 1
REC = 4
EMPTY_ROW = P * K
LN_EPS = 1e-5
NORM_EPS = 1e-12
CREDIT = SLOTS * GROUP
SPLIT = ((0, 112), (112, NA))
N_STORES = 4
EDGE_CONSTS, IDENT_CONSTS, CONSTS = 5, 8, 17
N_WEIGHTS = 3 * 2 + 2 + 2
assert K == GROUP * SLOTS * TURNS and NA * NB == NODES and GROUPS == TURNS * SLOTS and TURNS == 2 * HALF + 1
assert all(sum(kn for _, kn in LANDS[kind]) == GROUP - PE_STEPS[kind] for kind in LANDS)
assert all(len(LANDS[kind]) == PE_STEPS[kind] and min(kn for _, kn in LANDS[kind]) >= HOT_PIECES for kind in LANDS)
assert PIECE * PIECES == HI * LO


class Steps:

    def __init__(self):
        self.base, self.here, self.i, self.per = 0, 0, None, 0

    def loop(self, i, per):
        self.base, self.here, self.i, self.per = self.base + self.here, 0, i, per

    def end_loop(self, turns):
        assert self.here == self.per, (self.here, self.per)
        self.base, self.here, self.i = self.base + turns * self.per, 0, None

    def next(self):
        self.here += 1
        return self.base + self.here if self.i is None else self.i * self.per + (self.base + self.here)


def build(nc, x, src, dst, edge_type_8, W_l1, W_r1, sb1, W_l2, W_r2, sb2, w1, sl1, rb1, w2, sl2, rb2, out):
    with ExitStack() as ctx:
        def sb(name, shape, dt=F32):
            return ctx.enter_context(nc.sbuf_tensor(name, shape, dt))

        def sem(name):
            return ctx.enter_context(nc.semaphore(name))

        def scratch(name, shape, dt=F32):
            return nc.dram_tensor(name, shape, dt).ap()

        table = [scratch("table0", (NODES, D)), scratch("table1", (NODES, D)),
                 scratch("table2", (NODES * RELS, D)), scratch("table3", (NODES * RELS, D))]
        sorted_d = scratch("sorted_d", (P * K, REC), I32)
        run_rows = [scratch(f"run_rows{l}", (P * K + 1, D)) for l in range(4)]
        end_d, start_d, end_idx_d = scratch("end_d", (HI * LO,)), scratch("start_d", (HI * LO,)), \
            scratch("end_idx_d", (HI * LO,), I32)

        src_t = sb("src_t", [P, K], I32)
        dst_t = sb("dst_t", [P, K], I32)
        typ_t = sb("typ_t", [P, K], I32)
        prev_last = sb("prev_last", [P, 1], I32)
        dst_hi = sb("dst_hi", [P, K], BF16)
        dst_lo = sb("dst_lo", [P, K], BF16)
        rel_idx = sb("rel_idx", [P, K], I32)
        same = typ_t[:, :].bitcast(F32)
        idx_ring = sb("idx_ring", [P, SLOTS, GROUP], I32)
        ring = sb("ring", [P, SLOTS, GROUP, D])
        spare = ring[:, 0, :, :].rearrange("p k d -> p (k d)")
        dst_f = spare[:, 0:K]
        rank = spare[:, K:2 * K]
        hot = spare[:, 2 * K:2 * K + CLASSES // 2].bitcast(BF16)
        x_all = sb("x_all", [NA, NB, D])
        self_all = sb("self_all", [NA, NB, D])
        ends = sb("ends", [NA, NB, D])
        end_idx = sb("end_idx", [NA, NB], I32)
        span = sb("span", [P, NB, NA], BF16)
        end_w = sb("end_w", [P, NB * D])
        start_w = sb("start_w", [P, HI * LO])
        h_all = end_w[0:NA, :].rearrange("p (b d) -> p b d", b=NB)
        hit_w = sb("hit_w", [P, K * REC])
        end_b, start_b, hit = end_w[:, 0:NODES], start_w[:, 0:NODES], hit_w[:, 0:NODES]
        dst_part = hit_w[:, 0:K].bitcast(I32)
        before_w = sb("before_w", [P, P], BF16)
        after_w = sb("after_w", [P, P], BF16)
        col = sb("col", [P, 1])
        pos = sb("pos", [P, 1], I32)
        record = sb("record", [P, REC], I32)
        hot_hi = sb("hot_hi", [P, HI, GROUP], BF16)
        hot_lo = sb("hot_lo", [P, LO, GROUP], BF16)
        class_no = sb("class_no", [P, LO, GROUP], BF16)
        lo_edge = sb("lo_edge", [P, 1])
        hi_edge = sb("hi_edge", [P, 1])
        ident = sb("ident", [P, P])
        ones = sb("ones", [P, P])
        upper = sb("upper", [HI, HI])
        hist = sb("hist", [HI, LO])
        cum = sb("cum", [HI, LO])
        hist_tmp = sb("hist_tmp", [HI, LO])
        hist_new = sb("hist_new", [HI, LO])
        hist_idx = sb("hist_idx", [HI, LO], I32)
        hist_base = sb("hist_base", [HI, 1])
        zero_row = sb("zero_row", [1, D])
        passes = sb("passes", [P, 1])
        passes_last = sb("passes_last", [P, 1])
        passes_w = sb("passes_w", [P, P])
        passes_b = sb("passes_b", [P, P])
        unsorted_p = sb("unsorted_p", [P, 2])
        unsorted_i = sb("unsorted_i", [1, 1], I32)
        carry_t = sb("carry_t", [P, P])
        carry = sb("carry", [P, D])
        carry_r = sb("carry_r", [P, D])
        carry_parts = sb("carry_parts", [P, 3, D], BF16)
        last_rows = sb("last_rows", [P, D])
        agg = sb("agg", [NA, BLK, D])
        agg_t = sb("agg_t", [P, BLK, P])
        o_t = sb("o_t", [NA, BLK, D])
        sq_t = sb("sq_t", [NA, BLK, D])
        cen = sb("cen", [NA, BLK, D])
        h_t = sb("h_t", [NA, BLK, D])
        h_tr = sb("h_tr", [P, BLK, P])
        res = cen
        st = sb("st", [NA, 4, BLK])
        xt_out = sb("xt_out", [NA, BLK, RELS * D])
        h_parts = xt_out[:, :, :].rearrange("p j c -> p (j c)").bitcast(BF16)[:, 0:NB * 3 * D] \
            .rearrange("p (b c d) -> p b c d", b=NB, c=3)
        src_hot = ends[:, :, :].rearrange("p b d -> p (b d)").bitcast(BF16) \
            .rearrange("p (o b e) -> p o b e", o=2, b=NB)
        tile_no = sb("tile_no", [NA, NB, P], BF16)
        lane_base = sb("lane_base", [NA, 1])
        src_off = sb("src_off", [NA, MAX_STEPS, P], BF16)
        src_cols = sb("src_cols", [P, SLOTS, MAX_STEPS])
        src_h = start_w[:, 0:2 * P].rearrange("p (o e) -> p o e", o=2)
        rel_rows = start_w[:, 2 * P:2 * P + 2 * RELS * D].rearrange("p (o r d) -> p o r d", o=2, r=RELS)
        edge_rel = sb("edge_rel", [P, SUM_STEPS], I32)
        rel_no = sb("rel_no", [P, RELS])
        rel_mask = sb("rel_mask", [P, SLOTS, SUM_STEPS, RELS])
        eps_c = sb("eps_c", [NA, 1])
        w_l = [None, sb("w_l1", [D, D]), sb("w_l2", [D, D])]
        w_self = [sb(f"w_self{t}", [D, D]) for t in range(4)]
        b_self = [sb(f"b_self{t}", [NA, D]) for t in range(4)]
        w_rel = [None, None, sb("w_rel2", [D, RELS, D]), sb("w_rel3", [D, RELS, D])]

        ps = ctx.enter_context(nc.psum_tensor("ps", [P, 8, 512], F32))
        flat = ps[:, :, :].rearrange("p b n -> p (b n)")
        ps_c = flat[:, 0:BLK * P].rearrange("p (j n) -> p j n", n=P)
        ps_t = flat[:, 1024:1024 + BLK * P].rearrange("p (j n) -> p j n", n=P)
        ps_o = flat[:, 2048:2048 + BLK * P].rearrange("p (j n) -> p j n", n=P)
        ps_xa, ps_xb = ps[:, 6, :], ps[:, 7, :]
        ps_rows = [flat[:, 1024 * s:1024 * s + MAX_STEPS * P].rearrange("p (m d) -> p m d", m=MAX_STEPS)
                   for s in range(SLOTS)]
        ps_src = flat[0:NA, 2048:2048 + MAX_STEPS * P].rearrange("p (m e) -> p m e", m=MAX_STEPS)
        ps_src_h = [ps[:, 2 + o, 0:P] for o in range(2)]
        rel_banks = (6, 0)
        ps_rel = [flat[:, 512 * b:512 * b + RELS * D].rearrange("p (r d) -> p r d", r=RELS) for b in rel_banks]
        ps_passes = ps[:, 6, 0:P]
        ps_hist = ps[0:HI, 6, 0:LO]
        ps_seen = flat[:, 0:CLASSES]
        ps_small = ps[:, 7, 0:8]

        edges_in = sem("edges_in")
        x_first_in = sem("x_first_in")
        x_in = sem("x_in")
        first_weights_in = sem("first_weights_in")
        weights_in = sem("weights_in")
        consts_ready = sem("consts_ready")
        vec = sem("vec")
        unsorted_ready = sem("unsorted_ready")
        check_sum = sem("check_sum")
        check_int = sem("check_int")
        sort_vec = sem("sort_vec")
        sort_begun = sem("sort_begun")
        classes_ready = sem("classes_ready")
        seen_cleared = sem("seen_cleared")
        hot_made = sem("hot_made")
        ranked = sem("ranked")
        rank_read = sem("rank_read")
        counted = sem("counted")
        record_ready = sem("record_ready")
        record_out = sem("record_out")
        record_free = sem("record_free")
        records_in = sem("records_in")
        edges_sorted = sem("edges_sorted")
        idx_ready = sem("idx_ready")
        idx_staged = sem("idx_staged")
        group_begun = sem("group_begun")
        landed = {kind: [[sem(f"landed_{kind}{s}{q}") for q in range(len(parts))] for s in range(SLOTS)]
                  for kind, parts in LANDS.items()}
        part0, part1, part2 = sem("part0"), sem("part1"), sem("part2")
        rest_ready = sem("rest_ready")
        src_staged = sem("src_staged")
        src_spread = sem("src_spread")
        off_ready = sem("off_ready")
        src_hot_made = sem("src_hot_made")
        rows_fetched = sem("rows_fetched")
        masks_made = sem("masks_made")
        edge_rel_ready = sem("edge_rel_ready")
        src_h_full = sem("src_h_full")
        src_h_sb = sem("src_h_sb")
        rel_full = sem("rel_full")
        rel_masked = sem("rel_masked")
        rel_summed = sem("rel_summed")
        scan_done = sem("scan_done")
        stored = [sem(f"stored{s}") for s in range(SLOTS)]
        hot_ready = sem("hot_ready")
        hist_part = sem("hist_part")
        hist_added = sem("hist_added")
        base_ready = sem("base_ready")
        tot_ready = sem("tot_ready")
        bounds_ready = sem("bounds_ready")
        bounds_out = sem("bounds_out")
        bounds_in = sem("bounds_in")
        idx_in = sem("idx_in")
        span_ready = sem("span_ready")
        passes_ready = sem("passes_ready")
        passes_bc = sem("passes_bc")
        last_copied = sem("last_copied")
        last_t = sem("last_t")
        carry_scanned = sem("carry_scanned")
        carry_back = sem("carry_back")
        carry_split = sem("carry_split")
        end_row = [sem(f"end_row{j}") for j in range(BLK)]
        zero_out = sem("zero_out")
        c_full = sem("c_full")
        agg_ready = sem("agg_ready")
        agg_t_full = sem("agg_t_full")
        agg_t_sb = sem("agg_t_sb")
        prod_full = sem("prod_full")
        prod_read = sem("prod_read")
        sq_ready = sem("sq_ready")
        root_ready = sem("root_ready")
        x_added = sem("x_added")
        h_ready = sem("h_ready")
        h_kept = sem("h_kept")
        h_t_full = sem("h_t_full")
        h_t_sb = sem("h_t_sb")
        self_full = sem("self_full")
        self_sb = sem("self_sb")
        xta_full, xta_sb = sem("xta_full"), sem("xta_sb")
        xtb_full, xtb_sb = sem("xtb_full"), sem("xtb_sb")
        xt_stored = [sem(f"xt_stored{j}") for j in range(BLK)]
        table_out = [sem(f"table_out{t}") for t in range(2)]
        res_ready = sem("res_ready")
        res_out = sem("res_out")

        def run_idx(l):
            return src_t if l < 2 else rel_idx

        def fetched_before(l):
            return GROUPS * sum(PE_STEPS[KIND[j]] for j in range(l))

        def fetch_no(l, g, m):
            return g * PE_STEPS[KIND[l]] + (fetched_before(l) + m)

        def sum_no(l, g, m):
            return g * SUM_STEPS + (fetched_before(l) - fetched_before(2) + m)

        def pipeline(eng, turn, steps=None, per=0, before_last=None):
            turn(None, None, 0)
            turn(None, 0, 1)
            with eng.Fori(0, BLKS - 2) as u:
                if steps:
                    steps.loop(u, per)
                turn(u, u + 1, u + 2)
                if steps:
                    steps.end_loop(BLKS - 2)
            turn(BLKS - 2, BLKS - 1, None)
            if before_last:
                before_last()
            turn(BLKS - 1, None, None)

        def unsorted(eng):
            eng.wait_ge(check_int, 1)
            return eng.value_load(unsorted_i[:, :], min_val=0, max_val=P * K)

        block = ctx.enter_context(nc.Block())

        @block.sync
        def _(sp):
            x_tiles = x.rearrange("(a b) d -> a b d", b=NB)
            for a, z in SPLIT:
                sp.dma_start(x_all[a:z, 0:BLK, :], x_tiles[a:z, 0:BLK, :]).then_inc(x_first_in, 16)
            for a, z in SPLIT:
                sp.dma_start(x_all[a:z, BLK:NB, :], x_tiles[a:z, BLK:NB, :]).then_inc(x_in, 16)
            sp.wait_ge(consts_ready, EDGE_CONSTS)
            for tile, d in ((dst_t, dst), (src_t, src), (typ_t, edge_type_8)):
                for a, z in ((0, 112), (112, P - 1)):
                    sp.dma_start(tile[a:z, :], d[a * K:z * K].rearrange("(p k) -> p k", k=K)).then_inc(edges_in, 16)
                sp.dma_start(tile[P - 1:P, 0:TAIL], d[(P - 1) * K:EDGES].rearrange("(p k) -> p k", p=1)).then_inc(edges_in, 16)
            sp.dma_start(prev_last[1:P, :], dst[0:(P - 1) * K].rearrange("(p k) -> p k", k=K)[:, K - 1:K],
                         allow_slow_non_contiguous=True).then_inc(edges_in, 16)

            def load_self(t, w, b, done):
                sp.dma_start(w_self[t][:, :], w).then_inc(done, 16)
                sp.dma_start(b_self[t][:, :], b.rearrange("(o d) -> o d", o=1).broadcast_to([NA, D])).then_inc(done, 16)

            load_self(0, W_r1, sb1, first_weights_in)

            def store_h(t):
                tab = table[t].rearrange("(a b) d -> a b d", b=NB)
                with sp.Fori(0, BLKS) as i:
                    sp.wait_ge(h_ready, i + (BLKS * t + 1))
                    for a, z in SPLIT:
                        sp.dma_start(tab[a:z, bass.ds(i * BLK, BLK), :], h_t[a:z, :, :]).then_inc(table_out[t], 16)

            def store_group(l, i, s):
                rows = run_rows[l][0:P * K, :].rearrange("(p k) d -> p k d", k=K)
                for k0, kn in STORES[KIND[l]]:
                    at = s * GROUP + k0
                    sp.wait_ge(scan_done, i * (SLOTS * GROUP) + (CREDIT + K * l + at + kn))
                    sp.dma_start(rows[:, bass.ds(i * (SLOTS * GROUP) + at, kn), :],
                                 ring[:, s, k0:k0 + kn, :]).then_inc(stored[s], 16)

            def store_runs(l, first=0, last=TURNS):
                with sp.Fori(first, last) as i:
                    for s in range(SLOTS):
                        store_group(l, i, s)

            def store_xt(t):
                tab = table[t].rearrange("(a b r) d -> a b (r d)", b=NB, r=RELS)
                with sp.Fori(0, BLKS) as i:
                    for j in range(BLK):
                        m = i * BLK + (NB * (t - 2) + j)
                        sp.wait_ge(xta_sb, m + 2)
                        sp.wait_ge(xtb_sb, m + 2)
                        for a, z in SPLIT:
                            sp.dma_start(tab[a:z, bass.ds(i * BLK + j, 1), :].rearrange("a o c -> a (o c)"),
                                         xt_out[a:z, j, :]).then_inc(xt_stored[j], 16)

            store_h(0)
            for t, w, b in ((1, W_r2, sb2), (2, sl1, rb1), (3, sl2, rb2)):
                load_self(t, w, b, weights_in)
            for t, w in ((1, W_l1), (2, W_l2)):
                sp.dma_start(w_l[t][:, :], w).then_inc(weights_in, 16)
            for t, w in ((2, w1), (3, w2)):
                sp.dma_start(w_rel[t][:, :, :], w.rearrange("r d e -> d r e")).then_inc(weights_in, 16)
            for l in range(4):
                sp.dma_start(run_rows[l][EMPTY_ROW:EMPTY_ROW + 1, :], zero_row[:, :]).then_inc(zero_out, 16)
            with sp.If(unsorted(sp) != 0):
                sp.wait_ge(record_free, K + 1)
                sp.dma_start(hit_w[:, :].bitcast(I32), sorted_d.rearrange("(p k) c -> p (k c)", k=K)).then_inc(records_in, 16)
                sp.dma_start(prev_last[1:P, :],
                             sorted_d[0:(P - 1) * K, :].rearrange("(p k) c -> p (k c)", k=K)[:, (K - 1) * REC:(K - 1) * REC + 1],
                             allow_slow_non_contiguous=True).then_inc(records_in, 16)
                sp.wait_ge(edges_sorted, 1)
            store_runs(0, 0, HALF)
            store_group(0, HALF, 0)
            sp.wait_ge(bounds_ready, 1)
            sp.dma_start(end_d.rearrange("(h l) -> h l", l=LO), cum[:, :]).then_inc(bounds_out, 16)
            sp.dma_start(start_d.rearrange("(h l) -> h l", l=LO), hist_tmp[:, :]).then_inc(bounds_out, 16)
            sp.dma_start(end_idx_d.rearrange("(h l) -> h l", l=LO), hist_idx[:, :]).then_inc(bounds_out, 16)
            store_group(0, HALF, 1)
            sp.wait_ge(bounds_out, 48)
            sp.dma_start(end_idx[:, :], end_idx_d[0:NODES].rearrange("(a b) -> a b", b=NB)).then_inc(idx_in, 16)
            with sp.Fori(HALF + 1, SPANS_TURN) as i:
                for s, (tile, d) in enumerate(((end_w, end_d), (start_w, start_d))):
                    store_group(0, i, s)
                    piece = bass.ds(i * PIECE - (HALF + 1) * PIECE, PIECE)
                    sp.dma_start(tile[:, piece],
                                 d[piece].rearrange("(o n) -> o n", o=1).broadcast_to([P, PIECE])).then_inc(bounds_in, 16)
            store_runs(0, SPANS_TURN, TURNS)
            store_h(1)
            store_runs(1)
            store_xt(2)
            store_runs(2)
            store_xt(3)
            store_runs(3)
            o = out.rearrange("(a b) d -> a b d", b=NB)
            with sp.Fori(0, BLKS) as i:
                sp.wait_ge(res_ready, i + 1)
                for a, z in SPLIT:
                    sp.dma_start(o[a:z, bass.ds(i * BLK, BLK), :], res[a:z, :, :]).then_inc(res_out, 16)
            sp.wait_ge(res_out, 32 * BLKS + 1)
            for t in range(2):
                sp.wait_ge(table_out[t], 32 * BLKS + 1)
            sp.wait_ge(zero_out, 64)
            for s in range(SLOTS):
                sp.wait_ge(stored[s], 16 * N_STORES * TURNS * 4 + 1)
            for j in range(BLK):
                sp.wait_ge(xt_stored[j], 32 * BLKS * 2 + 1)

        @block.gpsimd
        def _(pool):
            made = Steps()

            def const(instruction):
                instruction.then_inc(consts_ready, 1)
                pool.wait_ge(consts_ready, made.next())

            const(pool.memset(dst_t[96:P, :], float(NODES)))
            const(pool.memset(src_t[96:P, :], 0.0))
            const(pool.memset(typ_t[96:P, :], 0.0))
            const(pool.memset(prev_last[:, :], -1.0))
            const(pool.memset(zero_row[:, :], 0.0))
            assert made.here == EDGE_CONSTS
            const(pool.memset(eps_c[:, :], LN_EPS))
            const(pool.memset(ones[:, :], 1.0))
            const(pool.affine_select(out=ident[:, :], in_=ones[:, :], compare_op=ALU.is_equal, fill=0.0, base=0,
                                     pattern=[[-1, P]], channel_multiplier=1))
            assert made.here == IDENT_CONSTS
            const(pool.affine_select(out=upper[:, :], in_=ones[0:HI, 0:HI], compare_op=ALU.is_gt, fill=0.0, base=0,
                                     pattern=[[1, HI]], channel_multiplier=-1))
            const(pool.iota(class_no[:, :, :], pattern=[[1, LO], [0, GROUP]], base=0, channel_multiplier=0,
                            allow_small_or_imprecise_dtypes=True))
            const(pool.iota(lo_edge[:, :], pattern=[[0, 1]], base=0, channel_multiplier=K,
                            allow_small_or_imprecise_dtypes=True))
            const(pool.iota(hi_edge[:, :], pattern=[[0, 1]], base=K, channel_multiplier=K,
                            allow_small_or_imprecise_dtypes=True))
            const(pool.affine_select(out=before_w[:, :], in_=ones[:, :], compare_op=ALU.is_gt, fill=0.0, base=0,
                                     pattern=[[1, P]], channel_multiplier=-1))
            const(pool.affine_select(out=after_w[:, :], in_=ones[:, :], compare_op=ALU.is_ge, fill=0.0, base=0,
                                     pattern=[[-1, P]], channel_multiplier=1))
            const(pool.iota(tile_no[:, :, :], pattern=[[1, NB], [0, P]], base=0, channel_multiplier=0,
                            allow_small_or_imprecise_dtypes=True))
            const(pool.iota(rel_no[:, :], pattern=[[1, RELS]], base=0, channel_multiplier=0,
                            allow_small_or_imprecise_dtypes=True))
            const(pool.iota(lane_base[:, :], pattern=[[0, 1]], base=0, channel_multiplier=-NB,
                            allow_small_or_imprecise_dtypes=True))
            assert made.here == CONSTS

            def gather_runs(l):
                with pool.Fori(0, TURNS) as i:
                    for s in range(SLOTS):
                        g = i * SLOTS + s
                        pool.wait_ge(idx_staged, g + (SLOTS * TURNS * l + 1))
                        pool.wait_ge(stored[s], i * (16 * N_STORES) + (16 * N_STORES * TURNS * l + 1))
                        pool.wait_ge(scan_done, g * GROUP + (CREDIT + K * l - GROUP + 4))
                        pool.sem_inc(group_begun, 1)
                        for q, (k0, kn) in enumerate(LANDS[KIND[l]]):
                            for k in range(k0, k0 + kn):
                                pool.indirect_dma_start(
                                    out=ring[:, s, k, :], out_offset=None, in_=table[l],
                                    in_offset=bass.IndirectOffsetOnAxis(ap=idx_ring[:, s, k:k + 1], axis=0),
                                ).then_inc(landed[KIND[l]][s][q], 16)

            def gather_ends(l):
                for s in range(SLOTS):
                    pool.wait_ge(stored[s], 16 * N_STORES * TURNS * (l + 1) + 1)
                if l == 0:
                    pool.wait_ge(zero_out, 64)
                    pool.wait_ge(idx_in, 16)
                else:
                    pool.wait_ge(agg_ready, BLKS * l + 1)
                for b in range(NB):
                    i, j = b // BLK, b % BLK
                    if i:
                        pool.wait_ge(end_row[j], 16 * (BLKS * l + i))
                    pool.indirect_dma_start(
                        out=ends[:, b, :], out_offset=None, in_=run_rows[l],
                        in_offset=bass.IndirectOffsetOnAxis(ap=end_idx[:, b:b + 1], axis=0),
                    ).then_inc(end_row[j], 16)

            with pool.If(unsorted(pool) != 0):
                pool.wait_ge(part2, 1)
                pool.iota(end_w[:, 0:CLASSES], pattern=[[1, CLASSES]], base=0, channel_multiplier=0,
                          allow_small_or_imprecise_dtypes=True).then_inc(classes_ready, 1)
                with pool.Fori(0, K) as i:
                    pool.wait_ge(record_ready, i + 1)
                    pool.sem_inc(group_begun, 1)
                    pool.indirect_dma_start(
                        out=sorted_d, out_offset=bass.IndirectOffsetOnAxis(ap=pos[:, :], axis=0),
                        in_=record[:, :], in_offset=None).then_inc(record_out, 16)
                    pool.wait_ge(record_out, i * 16 + 16)
                    pool.sem_inc(record_free, 1)
                pool.wait_ge(edges_sorted, 1)
            for l in range(4):
                if l < 2:
                    pool.wait_ge(table_out[l], 32 * BLKS + 1)
                else:
                    for j in range(BLK):
                        pool.wait_ge(xt_stored[j], 32 * BLKS * (l - 1) + 1)
                gather_runs(l)
                gather_ends(l)

        @block.scalar
        def _(act):
            def split_h(t):
                act.wait_ge(h_kept, BLKS * (t + 1) + 1)
                if t >= 2:
                    for j in range(BLK):
                        act.wait_ge(xt_stored[j], 32 * BLKS * (t - 1) + 1)
                act.copy(h_parts[:, :, 0, :], h_all).then_inc(part0, 1)
                act.wait_ge(rest_ready, t + 1)
                act.copy(h_parts[:, :, 1, :], h_all).then_inc(part1, 1)

            def offsets(l, g):
                steps = PE_STEPS[KIND[l]]
                act.wait_ge(src_spread, g + (GROUPS * l + 1))
                act.wait_ge(src_hot_made, fetch_no(l, g, 0) + 1)
                act.activation(src_off[:, 0:steps, :], ps_src[:, 0:steps, :], ACT.Identity,
                               bias=lane_base[:, :]).then_inc(off_ready, 1)

            def pick_relations(l, g, s, m):
                n = sum_no(l, g, m)
                act.wait_ge(rel_full, n + 1)
                if m == 0:
                    act.wait_ge(masks_made, g + (GROUPS * (l - 2) + 1))
                act.wait_ge(rel_summed, n + 1)
                for r in range(RELS):
                    instruction = act.activation(rel_rows[:, m % 2, r, :], ps_rel[m % 2][:, r, :], ACT.Copy,
                                                 scale=rel_mask[:, s, m, r:r + 1])
                instruction.then_inc(rel_masked, 1)

            def serve_group(l, g, s, more):
                if l < 2:
                    offsets(l, g)
                    return
                for m in range(SUM_STEPS):
                    if m == SUM_STEPS - 1 and more:
                        offsets(l, g + 1)
                    act.wait_ge(src_h_full, sum_no(l, g, m) + 3)
                    act.copy(src_h[:, m % 2, :], ps_src_h[m % 2]).then_inc(src_h_sb, 1)
                    if m:
                        pick_relations(l, g, s, m - 1)
                pick_relations(l, g, s, SUM_STEPS - 1)

            def serve(l):
                if l >= 2:
                    offsets(l, 0)
                with act.Fori(0, TURNS - 1) as i:
                    for s in range(SLOTS):
                        serve_group(l, i * SLOTS + s, s, True)
                for s in range(SLOTS):
                    serve_group(l, (TURNS - 1) * SLOTS + s, s, s < SLOTS - 1)

            def blocks(t):
                per, base = {0: (1, 0), 1: (1, BLKS), 2: (2, 2 * BLKS)}.get(t, (0, 0))

                def copy_products(before, tiles):
                    for j in tiles:
                        m = before * BLK + (NB * (t - 2) + j)
                        act.wait_ge(xt_stored[j], before * 32 + (32 * BLKS * (t - 2) + 1))
                        for half, (full, copied) in enumerate(((xta_full, xta_sb), (xtb_full, xtb_sb))):
                            act.wait_ge(full, m + 1)
                            act.copy(xt_out[:, j, half * 512:half * 512 + 512],
                                     ps[0:NA, 6 + half, :]).then_inc(copied, 1)

                def root(k, r, layer_norm):
                    act.wait_ge(sq_ready, k * per + (base + r + 1))
                    if layer_norm:
                        act.activation(st[:, 2, :], st[:, 1, :], ACT.Sqrt, bias=eps_c[:, :],
                                       scale=1.0 / D).then_inc(root_ready, 1)
                    else:
                        act.activation(st[:, 2, :], st[:, 1, :], ACT.Sqrt).then_inc(root_ready, 1)

                def turn(before, k, ahead):
                    products = t >= 2 and before is not None
                    if k is not None and t in (0, 1, 2):
                        root(k, 0, t == 0)
                    if products:
                        copy_products(before, (0,))
                    if ahead is not None and t in (1, 2):
                        act.wait_ge(agg_t_full, ahead + (BLKS * (t - 1) + 1))
                        act.copy(agg_t[:, :, 0:NA], ps_t[:, :, 0:NA]).then_inc(agg_t_sb, 1)
                    if products:
                        copy_products(before, (1, 2))
                    if k is not None and t == 2:
                        root(k, 1, True)
                    if products:
                        copy_products(before, (3, 4))
                    if k is not None:
                        act.wait_ge(h_t_full, k + (BLKS * t + 2))
                        act.copy(h_tr[:, :, 0:NA], ps_t[:, :, 0:NA]).then_inc(h_t_sb, 1)
                        if t < 4:
                            act.copy(h_all[:, bass.ds(k * BLK, BLK), :], h_t[:, :, :]).then_inc(h_kept, 1)

                pipeline(act, turn)

            act.wait_ge(consts_ready, IDENT_CONSTS)
            blocks(0)
            act.wait_ge(consts_ready, CONSTS)
            for l in range(4):
                split_h(l)
                if l == 0:
                    with act.If(unsorted(act) != 0):
                        act.wait_ge(edges_sorted, 1)
                serve(l)
                if l < 3:
                    blocks(l + 1)

        @block.tensor
        def _(pe):
            def count_before():
                chunks = [(c, min(512, CLASSES - c)) for c in range(0, CLASSES, 512)]

                def add(weights, start):
                    for c, width in chunks:
                        mm = pe.matmul(ps_seen[:, c:c + width], weights[:, :], hot[:, c:c + width],
                                       start=start, stop=True, skip_group_check=True)
                    return mm

                pe.wait_ge(sort_begun, 1)
                add(before_w, True).then_inc(seen_cleared, 1)
                with pe.Fori(0, K) as i:
                    pe.wait_ge(hot_made, i + 1)
                    add(before_w, False).then_inc(ranked, 1)
                    pe.wait_ge(rank_read, i + 1)
                    add(after_w, False).then_inc(counted, 1)

            def count_group(c):
                pe.wait_ge(hot_ready, c * 2 + 2)
                pe.wait_ge(hist_added, c + 1)
                for k in range(GROUP):
                    mm = pe.matmul(ps_hist, hot_hi[:, :, k], hot_lo[:, :, k],
                                   start=(k == 0), stop=(k == GROUP - 1))
                mm.then_inc(hist_part, 1)

            def spread_sources(l, g, s):
                pe.wait_ge(src_staged, g + (GROUPS * l + 1))
                pe.wait_ge(off_ready, g + (GROUPS * l + 1))
                for m in range(PE_STEPS[KIND[l]]):
                    mm = pe.matmul(ps_src[:, m, :], src_cols[:, s, m:m + 1].broadcast_to([P, NA]), ident[:, :],
                                   start=True, stop=True)
                mm.then_inc(src_spread, 1)

            def times_relations(l, g, m):
                n = sum_no(l, g, m)
                pe.wait_ge(src_h_sb, n + 3)
                pe.wait_ge(rel_masked, n + 1)
                for r in range(0, RELS, 4):
                    mm = pe.matmul(ps[:, rel_banks[m % 2] + r // 4, :], src_h[:, m % 2, :],
                                   w_rel[l][:, r:r + 4, :].rearrange("d r e -> d (r e)"), start=True, stop=True)
                mm.then_inc(rel_full, 1)

            def fetch_group(l, g, s, more, counts=False):
                steps = PE_STEPS[KIND[l]]
                for m in range(steps):
                    if m == steps - 1 and more:
                        spread_sources(l, g + 1, 1 - s)
                    pe.wait_ge(src_hot_made, fetch_no(l, g, m) + 2)
                    if l < 2:
                        pe.wait_ge(scan_done, g * GROUP + (K * l + CREDIT - GROUP))
                    else:
                        pe.wait_ge(src_h_sb, sum_no(l, g, m) + 1)
                    for b in range(NB):
                        for part in range(3):
                            h, hot = h_parts[:, b, part, :], src_hot[:, (steps * s + m) % 2, b, :]
                            group = dict(start=(b == 0 and part == 0), stop=(b == NB - 1 and part == 2))
                            if l < 2:
                                mm = pe.matmul(ps_rows[s][:, m, :], hot, h, **group)
                            else:
                                mm = pe.matmul(ps_src_h[m % 2], h, hot, **group)
                    mm.then_inc(rows_fetched if l < 2 else src_h_full, 1)
                    if l >= 2 and m:
                        times_relations(l, g, m - 1)
                    if counts and m == 2:
                        count_group(g * 2)
                    if counts and m == 4:
                        count_group(g * 2 + 1)
                if l >= 2:
                    times_relations(l, g, steps - 1)

            def fetch(l):
                pe.wait_ge(part2, l + 1)
                pe.wait_ge(self_sb, BLKS * (l + 1) + 1)
                pe.wait_ge(h_t_sb, BLKS * (l + 1))
                if l >= 2:
                    pe.wait_ge(xta_sb, NB * (l - 1) + 1)
                    pe.wait_ge(xtb_sb, NB * (l - 1) + 1)
                spread_sources(l, 0, 0)
                if l == 0:
                    with pe.Fori(0, HALF) as i:
                        for s in range(SLOTS):
                            fetch_group(l, i * SLOTS + s, s, True, counts=True)
                    fetch_group(l, HALF * SLOTS, 0, True, counts=True)
                    pe.wait_ge(tot_ready, 1)
                    pe.matmul(ps_small[0:HI, 0:1], upper[:, :], cum[:, LO - 1:LO],
                              start=True, stop=True).then_inc(base_ready, 1)
                    fetch_group(l, HALF * SLOTS + 1, 1, True)
                with pe.Fori(HALF + 1 if l == 0 else 0, TURNS - 1) as i:
                    for s in range(SLOTS):
                        fetch_group(l, i * SLOTS + s, s, True)
                for s in range(SLOTS):
                    fetch_group(l, (TURNS - 1) * SLOTS + s, s, s < SLOTS - 1)

            def carries(l):
                pe.wait_ge(last_copied, l + 1)
                pe.transpose(ps_t[:, 0, :], last_rows[:, :], ident[:, :]).then_inc(last_t, 1)
                pe.wait_ge(carry_scanned, l + 1)
                pe.transpose(ps_t[:, 1, :], carry_t[:, :], ident[:, :]).then_inc(carry_back, 1)
                pe.wait_ge(carry_split, l + 1)

            def blocks(t):
                def self_product(before, k):
                    if t == 0:
                        pe.wait_ge(first_weights_in, 32)
                    if k is not None and t in (1, 2):
                        pe.wait_ge(prod_read, k + (BLKS * (t - 1) + 1))
                    pe.wait_ge(h_t_sb, before + (BLKS * t + 1))
                    pe.wait_ge(self_sb, before + (BLKS * t + 1))
                    for j in range(BLK):
                        mm = pe.matmul(ps_o[0:NA, j, :], h_tr[:, j, 0:NA], w_self[t][:, :],
                                       start=True, stop=True)
                    mm.then_inc(self_full, 1)

                def products(before, tiles):
                    for j in tiles:
                        m = before * BLK + (NB * (t - 2) + j)
                        for half, (full, copied) in enumerate(((xta_full, xta_sb), (xtb_full, xtb_sb))):
                            pe.wait_ge(copied, m + 1)
                            pe.matmul(ps[0:NA, 6 + half, :], h_tr[:, j, 0:NA],
                                      w_rel[t][:, 4 * half:4 * half + 4, :].rearrange("d r e -> d (r e)"),
                                      start=True, stop=True).then_inc(full, 1)

                def turn(before, k, ahead):
                    pending = t in (2, 3) and before is not None
                    if t == 0 and k is not None and ahead is None:
                        pe.wait_ge(unsorted_ready, 1)
                        pe.matmul(ps_small[0:1, 0:1], ones[:, 0:1], unsorted_p[:, 0:1],
                                  start=True, stop=True).then_inc(check_sum, 1)
                    if ahead is not None and t >= 1:
                        n = ahead + (BLKS * (t - 1) + 1)
                        pe.wait_ge(agg_ready, n)
                        for j in range(BLK):
                            for part in range(3):
                                mm = pe.matmul(ps_c[0:NA, j, :],
                                               span[:, bass.ds(ahead * BLK + j, 1), :].rearrange("p o a -> p (o a)"),
                                               carry_parts[:, part, :], start=(part == 0), stop=(part == 2))
                        mm.then_inc(c_full, 1)
                    if before is not None and t < 4:
                        self_product(before, k)
                    if pending:
                        products(before, (0,))
                    if ahead is not None and t in (1, 2):
                        pe.wait_ge(agg_ready, n + 1)
                        for j in range(BLK):
                            mm = pe.transpose(ps_t[:, j, 0:NA], agg[:, j, :], ident[0:NA, 0:NA])
                        mm.then_inc(agg_t_full, 1)
                    if pending:
                        products(before, (1,))
                    if ahead is not None and t in (1, 2):
                        pe.wait_ge(agg_t_sb, n)
                        pe.wait_ge(self_sb, BLKS * t + 1 if before is None else before + (BLKS * t + 2))
                        if k is not None:
                            pe.wait_ge(prod_read, k + (BLKS * (t - 1) + 1))
                        for j in range(BLK):
                            mm = pe.matmul(ps_o[0:NA, j, :], agg_t[:, j, 0:NA], w_l[t][:, :], start=True, stop=True)
                        mm.then_inc(prod_full, 1)
                    if pending:
                        products(before, (2, 3, 4))
                    if k is not None and t < 4:
                        pe.wait_ge(h_ready, k + (BLKS * t + 1))
                        for j in range(BLK):
                            mm = pe.transpose(ps_t[:, j, 0:NA], h_t[:, j, :], ident[0:NA, 0:NA])
                        mm.then_inc(h_t_full, 1)

                pipeline(pe, turn)

            pe.wait_ge(consts_ready, IDENT_CONSTS)
            blocks(0)
            pe.wait_ge(consts_ready, CONSTS)
            pe.wait_ge(weights_in, 16 * N_WEIGHTS)
            with pe.If(unsorted(pe) != 0):
                count_before()
                pe.wait_ge(edges_sorted, 1)
            pe.wait_ge(passes_ready, 1)
            pe.matmul(ps_passes, passes_w[:, :], ident[:, :], start=True, stop=True).then_inc(passes_bc, 1)
            fetch(0)
            for t in range(1, 5):
                carries(t - 1)
                if t == 1:
                    pe.wait_ge(span_ready, 1)
                blocks(t)
                if t < 4:
                    fetch(t)

        @block.vector
        def _(dve):
            v = Steps()

            def step(instruction):
                instruction.then_inc(vec, 1)
                dve.wait_ge(vec, v.next())

            def over(column):
                return column.unsqueeze(2).broadcast_to([NA, BLK, D])

            def check_order():
                dve.wait_ge(edges_in, 16 * 10)
                step(dve.tensor_tensor(hit_w[:, 0:K - 1], dst_t[:, 1:K], dst_t[:, 0:K - 1], ALU.is_lt))
                step(dve.tensor_reduce(unsorted_p[:, 0:1], hit_w[:, 0:K - 1], AX.X, ALU.add))
                step(dve.tensor_tensor(unsorted_p[:, 1:2], dst_t[:, 0:1], prev_last[:, :], ALU.is_lt))
                dve.tensor_tensor(unsorted_p[:, 0:1], unsorted_p[:, 0:1], unsorted_p[:, 1:2], ALU.add).then_inc(unsorted_ready, 1)

            def stage_first(t):
                if t == 0:
                    with dve.If(unsorted(dve) == 0):
                        stage(0, 0, 0)
                        stage(0, 1, 1)
                elif t < 4:
                    stage(t, 0, 0)
                    stage(t, 1, 1)

            def blocks(t):
                op = ALU.max if t < 3 else ALU.add

                def add_carries(ahead):
                    for j in range(BLK):
                        dve.wait_ge(end_row[j], ahead * 16 + 16 * (BLKS * (t - 1) + 1))
                    dve.wait_ge(c_full, ahead + (BLKS * (t - 1) + 1))
                    dve.tensor_tensor(agg[:, :, :], ends[:, bass.ds(ahead * BLK, BLK), :], ps_c[0:NA, :, :],
                                      op).then_inc(agg_ready, 1)

                def add_self(before):
                    if t == 0:
                        dve.wait_ge(first_weights_in, 32)
                    else:
                        dve.wait_ge(weights_in, 16 * N_WEIGHTS)
                    dve.wait_ge(self_full, before + (BLKS * t + 1))
                    dve.tensor_tensor(self_all[:, bass.ds(before * BLK, BLK), :], ps_o[0:NA, :, :],
                                      b_self[t][:, :].unsqueeze(1).broadcast_to([NA, BLK, D]),
                                      ALU.add).then_inc(self_sb, 1)
                    dve.wait_ge(self_sb, before + (BLKS * t + 2))

                def turn(before, k, ahead):
                    roots = {0: (1, 0), 1: (1, BLKS), 2: (2, 2 * BLKS)}.get(t)

                    def others():
                        if ahead is not None and t >= 1:
                            add_carries(ahead)
                        if before is not None and t < 4:
                            add_self(before)

                    if k is None:
                        others()
                        return
                    tiles = bass.ds(k * BLK, BLK)
                    xs, selfs = x_all[:, tiles, :], self_all[:, tiles, :]
                    n = k + (BLKS * (t - 1) + 1)
                    if t in (1, 2):
                        dve.wait_ge(prod_full, n)
                        dve.wait_ge(h_ready, k + BLKS * t)
                        dve.tensor_tensor(o_t[:, :, :], ps_o[0:NA, :, :], selfs, ALU.add).then_inc(prod_read, 1)
                        dve.wait_ge(prod_read, n)
                        step(dve.tensor_tensor(sq_t[:, :, :], o_t[:, :, :], o_t[:, :, :], ALU.mult))
                        dve.tensor_reduce(st[:, 1, :], sq_t[:, :, :], AX.X, ALU.add).then_inc(sq_ready, 1)
                        others()
                        dve.wait_ge(root_ready, k * roots[0] + (roots[1] + 1))
                        step(dve.tensor_scalar(st[:, 3, :], st[:, 2, :], NORM_EPS, None, ALU.max))
                        step(dve.reciprocal(st[:, 3, :], st[:, 3, :]))
                    if t == 2:
                        step(dve.scalar_tensor_tensor(out=o_t[:, :, :], in0=o_t[:, :, :], scalar=0.0,
                                                      in1=over(st[:, 3, :]), op0=ALU.max, op1=ALU.mult))
                        step(dve.tensor_tensor(xs, xs, o_t[:, :, :], ALU.add))
                        dve.sem_inc(x_added, 1)
                    if t in (0, 2):
                        if t == 0:
                            dve.wait_ge(x_first_in if before is None else x_in, 32)
                        step(dve.tensor_reduce(st[:, 0, :], xs, AX.X, ALU.add))
                        step(dve.tensor_scalar(st[:, 0, :], st[:, 0, :], -1.0 / D, None, ALU.mult))
                        step(dve.tensor_tensor(cen[:, :, :], xs, over(st[:, 0, :]), ALU.add))
                        step(dve.tensor_tensor(sq_t[:, :, :], cen[:, :, :], cen[:, :, :], ALU.mult))
                        dve.tensor_reduce(st[:, 1, :], sq_t[:, :, :], AX.X, ALU.add).then_inc(sq_ready, 1)
                        dve.wait_ge(root_ready, k * roots[0] + (roots[1] + roots[0]))
                        step(dve.reciprocal(st[:, 3, :], st[:, 2, :]))
                    if t in (3, 4):
                        dve.wait_ge(agg_ready, n + 1)
                        step(dve.tensor_tensor(o_t[:, :, :], agg[:, :, :], selfs, ALU.add))
                    if t < 4:
                        dve.wait_ge(h_t_full, k + (BLKS * t + 1))
                        dve.wait_ge(h_kept, k + (BLKS * t + 1))
                        if t < 2:
                            dve.wait_ge(table_out[t], k * 32 + 1)
                        if t == 3:
                            dve.tensor_scalar(h_t[:, :, :], o_t[:, :, :], 0.0, None, ALU.max).then_inc(h_ready, 1)
                        else:
                            raw = o_t if t == 1 else cen
                            dve.scalar_tensor_tensor(out=h_t[:, :, :], in0=raw[:, :, :], scalar=0.0,
                                                     in1=over(st[:, 3, :]), op0=ALU.max,
                                                     op1=ALU.mult).then_inc(h_ready, 1)
                    if t == 4:
                        dve.wait_ge(res_out, k * 32 + 1)
                        dve.scalar_tensor_tensor(out=res[:, :, :], in0=o_t[:, :, :], scalar=0.0, in1=xs,
                                                 op0=ALU.max, op1=ALU.add).then_inc(res_ready, 1)
                    if t in (0, 3, 4):
                        others()
                    if t == 0 and before is None:
                        check_order()
                    if t == 0 and ahead is None:
                        dve.wait_ge(check_sum, 1)
                        dve.tensor_copy(unsorted_i[:, :], ps_small[0:1, 0:1]).then_inc(check_int, 1)

                pipeline(dve, turn, v, {0: 5, 1: 3, 2: 10, 3: 1, 4: 1}[t], lambda: stage_first(t))

            def split_h(t):
                dve.wait_ge(part0, t + 1)
                dve.tensor_tensor(h_all, h_all, h_parts[:, :, 0, :], ALU.subtract).then_inc(rest_ready, 1)
                dve.wait_ge(part1, t + 1)
                dve.tensor_tensor(h_parts[:, :, 2, :], h_all, h_parts[:, :, 1, :], ALU.subtract).then_inc(part2, 1)

            def one_hots(g):
                dve.wait_ge(hist_part, g + 1)
                for hot, part, n in ((hot_hi, dst_hi, HI), (hot_lo, dst_lo, LO)):
                    dve.tensor_tensor(hot[:, :, :],
                                      part[:, bass.ds(g * GROUP, GROUP)].unsqueeze(1).broadcast_to([P, n, GROUP]),
                                      class_no[:, 0:n, :], ALU.is_equal).then_inc(hot_ready, 1)

            def scan_steps(l, g, s, k0, kn, meanwhile=None):
                first = GROUP - MAX_STEPS
                for k in range(k0, k0 + kn):
                    before = ring[:, s, k - 1, :] if k else ring[:, 1 - s, GROUP - 1, :]
                    row = ring[:, s, k, :]
                    if l < 2 and k >= first:
                        m = BANK_STEPS - 1 if k - first < BANK_STEPS else MAX_STEPS - 1
                        dve.wait_ge(rows_fetched, fetch_no(l, g, m) + 3)
                        row = ps_rows[s][:, k - first, :]
                    at = g * GROUP + k
                    dve.wait_ge(scan_done, at + (CREDIT + K * l))
                    dve.scalar_tensor_tensor(out=ring[:, s, k, :], in0=before, scalar=same[:, bass.ds(at, 1)],
                                             in1=row, op0=ALU.mult,
                                             op1=ALU.max if l < 2 else ALU.add).then_inc(scan_done, 1)
                    if meanwhile:
                        meanwhile(k - k0)

            def stage(l, g, s):
                steps = PE_STEPS[KIND[l]]
                dve.tensor_copy(idx_ring[:, s, :], run_idx(l)[:, bass.ds(g * GROUP, GROUP)]).then_inc(idx_staged, 1)
                dve.tensor_copy(src_cols[:, s, 0:steps],
                                src_t[:, bass.ds(g * GROUP + GROUP - steps, steps)]).then_inc(src_staged, 1)

            def scan_landed(l, i, s, q, meanwhile=None):
                kind = KIND[l]
                k0, kn = LANDS[kind][q]
                dve.wait_ge(landed[kind][s][q], i * (16 * kn) + 16 * kn * (TURNS * (l % 2) + 1))
                scan_steps(l, i * SLOTS + s, s, k0, kn, meanwhile)

            def hot_sources(l, g, s, m, pieces=range(HOT_PIECES)):
                for j in pieces:
                    if j == 0:
                        dve.wait_ge(off_ready, g + (GROUPS * l + 2))
                        if l < 2:
                            dve.wait_ge(rows_fetched, fetch_no(l, g, m) + 1)
                        else:
                            dve.wait_ge(src_h_full, sum_no(l, g, m) + 1)
                    n = NB // HOT_PIECES
                    piece = dve.tensor_tensor(src_hot[:, (PE_STEPS[KIND[l]] * s + m) % 2, j * n:(j + 1) * n, :],
                                              src_off[:, m, :].unsqueeze(1).broadcast_to([NA, n, P]),
                                              tile_no[:, j * n:(j + 1) * n, :], ALU.is_equal)
                    if j == HOT_PIECES - 1:
                        piece.then_inc(src_hot_made, 1)

            def scan_with_hots(l, i, s, q, ahead):
                g, m, steps = i * SLOTS + s, q + 2, PE_STEPS[KIND[l]]
                if m >= steps:
                    g, s_hot, m = g + 1, 1 - s, m - steps
                    if not ahead:
                        scan_landed(l, i, s, q)
                        return
                    if l >= 2 and m == 0:
                        relation_masks(l, g, s_hot)
                else:
                    s_hot = s

                def meanwhile(j):
                    if j < HOT_PIECES:
                        hot_sources(l, g, s_hot, m, (j,))

                scan_landed(l, i, s, q, meanwhile)

            def relation_masks(l, g, s):
                first = g * GROUP + (GROUP - SUM_STEPS)
                dve.tensor_scalar(edge_rel[:, :], rel_idx[:, bass.ds(first, SUM_STEPS)], RELS - 1, None,
                                  ALU.bitwise_and).then_inc(edge_rel_ready, 1)
                dve.wait_ge(edge_rel_ready, g + (GROUPS * (l - 2) + 1))
                dve.tensor_tensor(rel_mask[:, s, :, :], edge_rel[:, :].unsqueeze(2).broadcast_to([P, SUM_STEPS, RELS]),
                                  rel_no[:, :].unsqueeze(1).broadcast_to([P, SUM_STEPS, RELS]),
                                  ALU.is_equal).then_inc(masks_made, 1)

            def sum_relations(l, g, s, m):
                dve.wait_ge(rel_masked, sum_no(l, g, m) + 3)
                dve.tensor_reduce(ring[:, s, GROUP - SUM_STEPS + m, :],
                                  rel_rows[:, m % 2, :, :].rearrange("p r d -> p d r"), AX.X,
                                  ALU.add).then_inc(rel_summed, 1)

            def add_histogram(c):
                dve.wait_ge(hist_part, c + 2)
                dve.tensor_tensor(hist[:, :], hist[:, :], ps_hist, ALU.add).then_inc(hist_added, 1)
                dve.wait_ge(hist_added, c + 2)

            def scan_max_group(l, i, s, ahead=SLOTS, counts=False):
                g = i * SLOTS + s
                for q in range(len(LANDS["max"])):
                    scan_with_hots(l, i, s, q, ahead)
                    if counts and q == 0:
                        one_hots(g * 2)
                    if counts and q == 2:
                        add_histogram(g * 2)
                        one_hots(g * 2 + 1)
                if counts:
                    add_histogram(g * 2 + 1)
                scan_steps(l, g, s, GROUP - MAX_STEPS, MAX_STEPS)
                if ahead > 1:
                    stage(l, g + 2, s)

            def scan_max(l):
                if l:
                    dve.wait_ge(agg_ready, BLKS * l + 1)
                hot_sources(l, 0, 0, 0)
                hot_sources(l, 0, 0, 1)
                if l == 0:
                    with dve.Fori(0, HALF) as i:
                        for s in range(SLOTS):
                            scan_max_group(l, i, s, counts=True)
                    scan_max_group(l, HALF, 0, counts=True)
                    node_bounds()
                    scan_max_group(l, HALF, 1)
                    with dve.Fori(HALF + 1, SPANS_TURN) as i:
                        for s in range(SLOTS):
                            scan_max_group(l, i, s)
                    spans()
                with dve.Fori(SPANS_TURN if l == 0 else 0, TURNS - 1) as i:
                    for s in range(SLOTS):
                        scan_max_group(l, i, s)
                for s in range(SLOTS):
                    scan_max_group(l, TURNS - 1, s, SLOTS - 1 - s)

            def scan_sum_group(l, i, s, ahead=SLOTS):
                g = i * SLOTS + s
                for q in range(len(LANDS["sum"])):
                    scan_with_hots(l, i, s, q, ahead)
                    if q:
                        sum_relations(l, g, s, q - 1)
                sum_relations(l, g, s, SUM_STEPS - 1)
                dve.wait_ge(rel_summed, sum_no(l, g, SUM_STEPS) + 2)
                scan_steps(l, g, s, GROUP - SUM_STEPS, SUM_STEPS)
                if ahead > 1:
                    stage(l, g + 2, s)

            def scan_sum(l):
                dve.wait_ge(agg_ready, BLKS * l + 1)
                relation_masks(l, 0, 0)
                hot_sources(l, 0, 0, 0)
                hot_sources(l, 0, 0, 1)
                with dve.Fori(0, TURNS - 1) as i:
                    for s in range(SLOTS):
                        scan_sum_group(l, i, s)
                for s in range(SLOTS):
                    scan_sum_group(l, TURNS - 1, s, SLOTS - 1 - s)

            def keep_last(l):
                dve.wait_ge(scan_done, CREDIT + K * (l + 1))
                dve.tensor_copy(last_rows[:, :], ring[:, SLOTS - 1, GROUP - 1, :]).then_inc(last_copied, 1)

            def node_bounds():
                step(dve.tensor_tensor_scan(cum[:, :], ones[0:HI, 0:LO], hist[:, :], 0.0, ALU.mult, ALU.add))
                dve.sem_inc(tot_ready, 1)
                dve.wait_ge(base_ready, 1)
                step(dve.tensor_copy(hist_base[:, :], ps_small[0:HI, 0:1]))
                step(dve.tensor_scalar(cum[:, :], cum[:, :], hist_base[:, :], -1.0, ALU.add, ALU.add))
                step(dve.scalar_tensor_tensor(out=hist_tmp[:, :], in0=cum[:, :], scalar=1.0, in1=hist[:, :],
                                              op0=ALU.add, op1=ALU.subtract))
                step(dve.tensor_scalar(hist_new[:, :], cum[:, :], -1.0, float(EMPTY_ROW), ALU.mult, ALU.add))
                step(dve.scalar_tensor_tensor(out=hist_new[:, :], in0=hist[:, :], scalar=0.0, in1=hist_new[:, :],
                                              op0=ALU.is_equal, op1=ALU.mult))
                dve.tensor_tensor(hist_idx[:, :], hist_new[:, :], cum[:, :], ALU.add).then_inc(bounds_ready, 1)

            def spans():
                dve.wait_ge(bounds_in, 32 * PIECES)
                step(dve.tensor_scalar(hit, end_b, hi_edge[:, :], None, ALU.is_lt))
                step(dve.scalar_tensor_tensor(out=hit, in0=end_b, scalar=lo_edge[:, :], in1=hit,
                                              op0=ALU.is_ge, op1=ALU.mult))
                dve.scalar_tensor_tensor(out=span[:, :, :].rearrange("p b a -> p a b"),
                                         in0=start_b.rearrange("p (a b) -> p a b", b=NB),
                                         scalar=lo_edge[:, :],
                                         in1=hit.rearrange("p (a b) -> p a b", b=NB),
                                         op0=ALU.is_lt, op1=ALU.mult).then_inc(span_ready, 1)

            def carries(l):
                dve.wait_ge(last_t, l + 1)
                dve.tensor_tensor_scan(carry_t[:, 1:P], passes_b[:, 0:P - 1], ps_t[:, 0, 0:P - 1], 0.0,
                                       ALU.mult, ALU.max if l < 2 else ALU.add).then_inc(carry_scanned, 1)
                dve.wait_ge(carry_back, l + 1)
                step(dve.tensor_copy(carry_parts[:, 0, :], ps_t[:, 1, :]))
                step(dve.tensor_tensor(carry[:, :], ps_t[:, 1, :], carry_parts[:, 0, :], ALU.subtract))
                step(dve.tensor_copy(carry_parts[:, 1, :], carry[:, :]))
                step(dve.tensor_tensor(carry_r[:, :], carry[:, :], carry_parts[:, 1, :], ALU.subtract))
                dve.tensor_copy(carry_parts[:, 2, :], carry_r[:, :]).then_inc(carry_split, 1)

            def sort_edges():
                w = Steps()

                def sort_step(instruction):
                    instruction.then_inc(sort_vec, 1)
                    dve.wait_ge(sort_vec, w.next())

                dve.memset(hot[:, :], 0.0).then_inc(sort_begun, 1)
                sort_step(dve.tensor_copy(dst_f[:, :], dst_t[:, :]))
                dve.wait_ge(seen_cleared, 1)
                dve.wait_ge(classes_ready, 1)
                with dve.Fori(0, K) as i:
                    w.loop(i, 3)
                    dve.wait_ge(counted, i + 1)
                    dve.tensor_scalar(hot[:, :], end_w[:, 0:CLASSES], dst_f[:, bass.ds(i, 1)], None,
                                      ALU.is_equal).then_inc(hot_made, 1)
                    dve.wait_ge(hot_made, i + 1)
                    dve.wait_ge(ranked, i + 1)
                    sort_step(dve.tensor_tensor(hit_w[:, 0:CLASSES], ps_seen, hot[:, :], ALU.mult))
                    sort_step(dve.tensor_reduce(col[:, :], hit_w[:, 0:CLASSES], AX.X, ALU.add))
                    sort_step(dve.tensor_scalar(rank[:, bass.ds(i, 1)], col[:, :], 0.0, None, ALU.add))
                    dve.sem_inc(rank_read, 1)
                w.end_loop(K)
                dve.wait_ge(counted, K + 1)
                sort_step(dve.memset(hit_w[:, 0:CLASSES], 1.0))
                sort_step(dve.tensor_tensor_scan(start_w[:, 0:CLASSES], hit_w[:, 0:CLASSES], ps_seen, 0.0, ALU.mult, ALU.add))
                sort_step(dve.tensor_tensor(start_w[:, 0:CLASSES], start_w[:, 0:CLASSES], ps_seen, ALU.subtract))
                with dve.Fori(0, K) as i:
                    w.loop(i, 6)
                    sort_step(dve.scalar_tensor_tensor(out=hit_w[:, 0:CLASSES], in0=end_w[:, 0:CLASSES],
                                                  scalar=dst_f[:, bass.ds(i, 1)], in1=start_w[:, 0:CLASSES],
                                                  op0=ALU.is_equal, op1=ALU.mult))
                    sort_step(dve.tensor_reduce(col[:, :], hit_w[:, 0:CLASSES], AX.X, ALU.add))
                    dve.wait_ge(record_free, i + 1)
                    sort_step(dve.tensor_scalar(pos[:, :], rank[:, bass.ds(i, 1)], col[:, :], None, ALU.add))
                    for c, tile in enumerate((dst_t, src_t, typ_t)):
                        sort_step(dve.tensor_scalar(record[:, c:c + 1], tile[:, bass.ds(i, 1)], 0.0, None, ALU.add))
                    dve.sem_inc(record_ready, 1)
                w.end_loop(K)
                dve.wait_ge(records_in, 32)
                for c, tile in enumerate((dst_t, src_t, typ_t)):
                    sort_step(dve.tensor_copy(tile[:, :], hit_w[:, :].bitcast(I32).rearrange("p (k c) -> p k c", c=REC)[:, :, c]))
                dve.sem_inc(edges_sorted, 1)

            for free in (agg_ready, xta_sb, xtb_sb, h_t_full, table_out[0], table_out[1], res_out, hist_part,
                         hist_added, counted, record_free, self_sb, h_kept, *stored, *xt_stored):
                dve.sem_inc(free, 1)
            dve.sem_inc(scan_done, CREDIT)
            dve.sem_inc(off_ready, 1)
            dve.sem_inc(src_hot_made, 1)
            dve.sem_inc(rows_fetched, 2)
            dve.sem_inc(src_h_full, 2)
            dve.sem_inc(src_h_sb, 2)
            dve.sem_inc(rel_summed, 2)
            dve.sem_inc(rel_masked, 2)
            step(dve.memset(ring[:, SLOTS - 1, GROUP - 1, :], 0.0))
            step(dve.memset(hist[:, :], 0.0))
            step(dve.memset(carry_t[:, 0:1], 0.0))
            step(dve.memset(record[:, :], 0))

            blocks(0)

            dve.wait_ge(consts_ready, CONSTS)
            violations = unsorted(dve)
            with dve.If(violations != 0):
                split_h(0)
                sort_edges()
                stage(0, 0, 0)
                stage(0, 1, 1)
            with dve.If(violations == 0):
                split_h(0)
            dve.scalar_tensor_tensor(out=rel_idx[:, :], in0=src_t[:, :], scalar=float(RELS), in1=typ_t[:, :],
                                     op0=ALU.mult, op1=ALU.add).then_inc(idx_ready, 1)
            dve.wait_ge(idx_ready, 1)
            step(dve.memset(same[:, 0:1], 0.0))
            step(dve.tensor_tensor(same[:, 1:K], dst_t[:, 1:K], dst_t[:, 0:K - 1], ALU.is_equal))
            for part, operand, op in ((dst_hi, LO.bit_length() - 1, ALU.logical_shift_right), (dst_lo, LO - 1, ALU.bitwise_and)):
                step(dve.tensor_scalar(dst_part, dst_t[:, :], operand, None, op))
                step(dve.tensor_copy(part[:, :], dst_part))
            step(dve.tensor_tensor(passes[:, :], dst_t[:, 0:1], prev_last[:, :], ALU.is_equal))
            step(dve.tensor_copy(passes_last[:, :], dst_t[:, K - 1:K]))
            step(dve.scalar_tensor_tensor(out=passes[:, :], in0=dst_t[:, 0:1], scalar=passes_last[:, :],
                                          in1=passes[:, :], op0=ALU.is_equal, op1=ALU.mult))
            dve.tensor_scalar(passes_w[:, :], ones[:, :], passes[:, :], None, ALU.mult).then_inc(passes_ready, 1)
            dve.wait_ge(passes_bc, 1)
            step(dve.tensor_copy(passes_b[:, :], ps_passes))
            for l in range(4):
                if l < 2:
                    scan_max(l)
                else:
                    scan_sum(l)
                keep_last(l)
                carries(l)
                blocks(l + 1)
                if l < 3:
                    split_h(l + 1)


INPUTS = ["x", "src", "dst", "edge_type_8", "L0_gnn_W_l1", "L0_gnn_W_r1", "L0_gnn_b1", "L0_gnn_W_l2", "L0_gnn_W_r2",
          "L0_gnn_b2", "L1_gnn_w1", "L1_gnn_sl1", "L1_gnn_b1", "L1_gnn_w2", "L1_gnn_sl2", "L1_gnn_b2"]


def kernel(**inputs):
    import numpy as np
    import concourse.bacc as bacc
    from concourse.bass_utils import run_bass_kernel_spmd

    nc = bacc.Bacc("TRN2", target_bir_lowering=False, num_devices=1)
    arrays, args = {}, []
    for name in INPUTS:
        a = np.ascontiguousarray(inputs[name])
        arrays[f"in_{name}"] = a
        args.append(nc.dram_tensor(f"in_{name}", a.shape, mybir.dt.from_np(a.dtype), kind="ExternalInput").ap())
    out = nc.dram_tensor("out", (NODES, D), F32, kind="ExternalOutput").ap()
    build(nc, *args, out)
    return run_bass_kernel_spmd(nc, [arrays], core_ids=[0]).results[0]["out"]
```
